# Optimizing a Trainium2 kernel written in Bass

```python
import numpy as np
import jax
import jax.numpy as jnp

def _softmax(x, axis=-1):
    return jax.nn.softmax(x, axis=axis)
def _gelu(x):
    return jax.nn.gelu(x, approximate=True)
def _silu(x):
    return jax.nn.silu(x)
def _sigmoid(x):
    return jax.nn.sigmoid(x)
def _layernorm(x, axis=-1, eps=1e-5):
    m = jnp.mean(x, axis=axis, keepdims=True)
    v = jnp.var(x, axis=axis, keepdims=True)
    return (x - m) / jnp.sqrt(v + eps)
def _scatter_add(tgt, idx, src, axis=0):
    return tgt.at[idx].add(src)
def _segment_sum(src, seg, n):
    return jax.ops.segment_sum(src, seg, n)

kernel_name = 'mk_adj_resnorm_d2_adj_256_964279'

def setup_inputs(seed: int = 0):
    np.random.seed(seed)
    _w = jnp.asarray
    def _rec_inputs():
        import jax
        import jax.numpy as jnp
        _gk = jax.random.key(seed)
        x = -0.0002928 + 1 * jax.random.normal(jax.random.fold_in(_gk, 1), (16, 1024, 256), jnp.float32)
        _a = jax.random.bernoulli(jax.random.fold_in(_gk, 2), 0.0078125, (1024, 1024))
        _a = jnp.logical_or(_a, jnp.swapaxes(_a, -1, -2))
        _a = jnp.logical_or(_a, jnp.eye(1024, dtype=bool))
        adj = _a.astype(jnp.int32)
        return x, adj
    x, adj = _rec_inputs()
    def _L0_gnn_setup():
        import jax, jax.numpy as jnp
        import numpy as np
        B, N, F_IN, F_OUT = (8, 2048, 256, 256)
        key = jax.random.key(seed)
        k1, k2, k3, k4 = jax.random.split(key, 4)
        x = jax.random.normal(k1, (B, N, F_IN), dtype=jnp.float32)
        W = jax.random.normal(k2, (F_IN, F_OUT), dtype=jnp.float32) * (1.0 / np.sqrt(F_IN))
        a = jax.random.normal(k3, (2 * F_OUT, 1), dtype=jnp.float32) * (1.0 / np.sqrt(2 * F_OUT))
        adj = jax.random.randint(k4, (N, N), 0, 2, dtype=jnp.int32)
        return {'x': x, 'W': W, 'a': a, 'adj': adj}
    _L0_gnn_all = _L0_gnn_setup()
    _L0_gnn_in = {k: v for k, v in _L0_gnn_all.items() if k in ('W', 'a', )}
    del _L0_gnn_all

    def _L1_gnn_setup():
        import jax, jax.numpy as jnp
        import numpy as np
        ALPHA = 0.2
        NEG_INF = -9000000000000000.0

        def _gat(inp, adj_mask, W, a):
            h = jnp.matmul(inp, W)
            F_ = h.shape[-1]
            f1 = jnp.matmul(h, a[:F_, 0])
            f2 = jnp.matmul(h, a[F_:, 0])
            e = jax.nn.leaky_relu(f1[:, :, None] + f2[:, None, :], ALPHA)
            if adj_mask is not None:
                e = jnp.where(adj_mask[None, :, :] > 0, e, NEG_INF)
            att = jax.nn.softmax(e, axis=2)
            h_prime = jnp.einsum('bij,bjf->bif', att, h)
            return jax.nn.elu(h_prime)
        key = jax.random.key(seed)
        ks = jax.random.split(key, 10)
        B, N, Fin, H, O = (16, 1024, 256, 512, 256)

        def xavier(k, shape):
            fan_in, fan_out = (shape[0], shape[-1])
            bound = 1.414 * np.sqrt(6.0 / (fan_in + fan_out))
            return jax.random.uniform(k, shape, jnp.float32, -bound, bound)
        return {'x': jax.random.normal(ks[0], (B, N, Fin), jnp.float32), 'adj': jax.random.randint(ks[1], (N, N), 0, 2, jnp.int32), 'mlp1_w': xavier(ks[2], (Fin, H)), 'mlp1_b': jnp.zeros((H,), jnp.float32), 'mlp2_w': xavier(ks[3], (H, O)), 'mlp2_b': jnp.zeros((O,), jnp.float32), 'W_fc': xavier(ks[4], (H, H)), 'a_fc': xavier(ks[5], (2 * H, 1)), 'W_hand': xavier(ks[6], (O, O)), 'a_hand': xavier(ks[7], (2 * O, 1))}
    _L1_gnn_all = _L1_gnn_setup()
    _L1_gnn_in = {k: v for k, v in _L1_gnn_all.items() if k in ('mlp1_w', 'mlp1_b', 'mlp2_w', 'mlp2_b', 'W_fc', 'a_fc', 'W_hand', 'a_hand', )}
    del _L1_gnn_all

    return {
        "x": x,
        "adj": adj,
        "L0_gnn_W": _L0_gnn_in["W"],
        "L0_gnn_a": _L0_gnn_in["a"],
        "L1_gnn_mlp1_w": _L1_gnn_in["mlp1_w"],
        "L1_gnn_mlp1_b": _L1_gnn_in["mlp1_b"],
        "L1_gnn_mlp2_w": _L1_gnn_in["mlp2_w"],
        "L1_gnn_mlp2_b": _L1_gnn_in["mlp2_b"],
        "L1_gnn_W_fc": _L1_gnn_in["W_fc"],
        "L1_gnn_a_fc": _L1_gnn_in["a_fc"],
        "L1_gnn_W_hand": _L1_gnn_in["W_hand"],
        "L1_gnn_a_hand": _L1_gnn_in["a_hand"],
    }

def reference(x, adj, L0_gnn_W, L0_gnn_a, L1_gnn_mlp1_w, L1_gnn_mlp1_b, L1_gnn_mlp2_w, L1_gnn_mlp2_b, L1_gnn_W_fc, L1_gnn_a_fc, L1_gnn_W_hand, L1_gnn_a_hand):
    import jax
    import jax.numpy as jnp
    def _L0_gnn_ref(x, W, a, adj):
        import jax, jax.numpy as jnp
        import numpy as np
        B, N, F_IN, F_OUT = (8, 2048, 256, 256)
        h = jnp.einsum('bnf,fo->bno', x, W)
        F = W.shape[1]
        a1 = a[:F, 0]
        a2 = a[F:, 0]
        s1 = jnp.einsum('bno,o->bn', h, a1)
        s2 = jnp.einsum('bno,o->bn', h, a2)
        e = jax.nn.leaky_relu(s1[:, :, None] + s2[:, None, :], negative_slope=0.2)
        mask = adj.astype(h.dtype)[None, :, :]
        e = e + (1.0 - mask) * -1000000000.0
        attention = jax.nn.softmax(e, axis=-1)
        out = jnp.einsum('bnm,bmo->bno', attention, h)
        return out

    def _L1_gnn_ref(x, adj, mlp1_w, mlp1_b, mlp2_w, mlp2_b, W_fc, a_fc, W_hand, a_hand):
        import jax, jax.numpy as jnp
        import numpy as np
        ALPHA = 0.2
        NEG_INF = -9000000000000000.0

        def _gat(inp, adj_mask, W, a):
            h = jnp.matmul(inp, W)
            F_ = h.shape[-1]
            f1 = jnp.matmul(h, a[:F_, 0])
            f2 = jnp.matmul(h, a[F_:, 0])
            e = jax.nn.leaky_relu(f1[:, :, None] + f2[:, None, :], ALPHA)
            if adj_mask is not None:
                e = jnp.where(adj_mask[None, :, :] > 0, e, NEG_INF)
            att = jax.nn.softmax(e, axis=2)
            h_prime = jnp.einsum('bij,bjf->bif', att, h)
            return jax.nn.elu(h_prime)
        out = jax.nn.relu(jnp.matmul(x, mlp1_w) + mlp1_b)
        residual = out
        out = _gat(jax.nn.relu(out), None, W_fc, a_fc)
        out = jax.nn.elu(out) + residual
        out = jax.nn.relu(jnp.matmul(out, mlp2_w) + mlp2_b)
        residual = out
        out = _gat(jax.nn.relu(out), adj, W_hand, a_hand)
        out = jax.nn.elu(out) + residual
        return jax.nn.relu(out)

    x = _layernorm(x + _L0_gnn_ref(x, L0_gnn_W, L0_gnn_a, adj), axis=-1)
    x = _layernorm(x + _L1_gnn_ref(x, adj, L1_gnn_mlp1_w, L1_gnn_mlp1_b, L1_gnn_mlp2_w, L1_gnn_mlp2_b, L1_gnn_W_fc, L1_gnn_a_fc, L1_gnn_W_hand, L1_gnn_a_hand), axis=-1)
    return x


_drawn_inputs = setup_inputs


def setup_inputs(seed=0):
    import zlib

    import numpy as np

    out = dict(_drawn_inputs(seed))
    spreads = {'L1_gnn_mlp1_b': (0.0, 0.1), 'L1_gnn_mlp2_b': (0.0, 0.1)}
    factors = {}
    for name, (base, spread) in spreads.items():
        noise = np.random.default_rng([zlib.crc32(name.encode()), seed]).standard_normal(out[name].shape)
        drawn = base * np.exp(spread * noise) if base else spread * noise
        out[name] = jnp.asarray(drawn.astype(out[name].dtype))
    for name, factor in factors.items():
        out[name] = (out[name] * factor).astype(out[name].dtype)
    return out
```

```python
from contextlib import ExitStack

import concourse.bass as bass
import concourse.mybir as mybir

F32 = mybir.dt.float32
F32R = mybir.dt.float32r
BF16 = mybir.dt.bfloat16
I32 = mybir.dt.int32
ACT = mybir.ActivationFunctionType
ALU = mybir.AluOpType
AX = mybir.AxisListType

P = 128
SLOPE = 0.2
MASKED = -9e15
EPS = 1e-5
LOWEST = -3.0e38

ADDS = {
    "A": dict(tile=8, masked=0, elu=8, resid=0, unit=8, pairs=4, split=0, fc=0, g0=0, hand=0),
    "B": dict(tile=8, masked=8, elu=0, resid=0, unit=0, pairs=0, split=0, fc=0, g0=0, hand=0),
    "C": dict(tile=0, masked=0, elu=0, resid=0, unit=18, pairs=9, split=8, fc=0, g0=0, hand=1),
    "D": dict(tile=0, masked=0, elu=0, resid=0, unit=24, pairs=12, split=8, fc=1, g0=0, hand=0),
    "E": dict(tile=8, masked=8, elu=8, resid=8, unit=0, pairs=0, split=0, fc=0, g0=0, hand=0),
    "F": dict(tile=0, masked=0, elu=0, resid=0, unit=14, pairs=7, split=8, fc=0, g0=1, hand=0),
}
NAMES = list(ADDS["A"])


class At:

    def __init__(self, counts, batch):
        self.counts, self.batch = counts, batch

    def __getattr__(self, name):
        return self.counts[name]


def add(counts, phases):
    return {n: counts[n] + sum(ADDS[p][n] for p in phases) for n in NAMES}


def walk(eng, batches, phase, ahead):
    zero = {n: 0 for n in NAMES}

    def steps(counts, k, body):
        done = []
        for item in body:
            name, shift, nxt = item
            at = At(add(counts, done), k + shift)
            if name == "ahead":
                ahead(nxt, at)
            else:
                phase(name, at, nxt)
                done.append(name)

    first = [("F", 0, None), ("ahead", 0, "B"), ("B", 0, None), ("D", 0, None), ("ahead", 0, "A"), ("F", 1, None)]
    body = [("A", 0, "B"), ("B", 1, None), ("C", 0, None), ("ahead", 0, "E"), ("D", 1, None), ("E", 0, "A"), ("F", 2, None)]
    steps(zero, 0, first)
    start = add(zero, "FBDF")
    per = add(zero, "ABCDEF")
    with eng.Fori(0, batches - 2) as k:
        steps({n: k * per[n] + start[n] for n in NAMES}, k, body)
    last = {n: (batches - 2) * per[n] + start[n] for n in NAMES}
    steps(last, batches - 2, body[:-1])
    steps(add(last, "ABCDE"), batches - 1, [("A", 0, None), ("C", 0, None), ("ahead", 0, "E"), ("E", 0, None)])


def wait(eng, sem, value):
    if isinstance(value, int) and value <= 0:
        return
    eng.wait_ge(sem, value)


def build(nc, x, adj, w0, a0, w1, b1, w2, b2, wfc, afc, wh, ah, out):
    batches, tokens, feat = x.shape
    hid = w1.shape[1]
    NT = tokens // P
    KF = feat // P
    KH = hid // P
    HALF = tokens // 2
    assert (NT, KF, KH, HALF) == (8, 2, 4, 512)
    G0, FC, HAND = 0, 1, 2
    LAYER = {"A": FC, "B": G0, "E": HAND}
    WIDTH = {"A": hid, "B": feat, "E": feat}

    ctx = ExitStack()
    with ctx:
        def sb(name, shape, dt=F32):
            return ctx.enter_context(nc.sbuf_tensor(name, shape, dt))

        def pb(name, shape):
            return ctx.enter_context(nc.psum_tensor(name, shape, F32))

        def sem(name):
            return ctx.enter_context(nc.semaphore(name))

        w0e = sb("w0e", [P, KF, feat + 3])
        w1s = sb("w1s", [P, KF, hid])
        wfcs = sb("wfcs", [P, KH, hid])
        wfa = sb("wfa", [P, KH, 3])
        w2s = sb("w2s", [P, KH, feat])
        whe = sb("whe", [P, KF, feat + 3])
        b1c = sb("b1c", [P, KH])
        b2c = sb("b2c", [P, KF])
        ident = sb("ident", [P, P])
        half_neg = sb("half_neg", [P, 1])
        eps = sb("eps", [P, 1])
        minus_one = sb("minus_one", [P, 1])
        mask_add = sb("mask_add", [P, NT, tokens], BF16)
        x_nat = sb("x_nat", [P, NT, feat])
        x1 = sb("x1", [P, NT, feat])
        x1_res = sb("x1_res", [P, NT, feat])
        o_nat = sb("o_nat", [P, NT, feat])
        h_wide = sb("h_wide", [P, 2, NT, hid], F32R)
        h_slim = sb("h_slim", [P, 2, NT, feat], F32R)
        H = {"A": h_wide, "B": h_slim, "E": h_slim}
        xT = sb("xT", [P, KF, tokens])
        rT = sb("rT", [P, KH, tokens])
        fcol = sb("fcol", [P, 3, NT, 3])
        f2b = sb("f2b", [P, 3, tokens])
        zbuf = sb("zbuf", [P, 2, tokens])
        prob = sb("prob", [P, 2, tokens])
        pT_hi = sb("pT_hi", [P, 2, tokens], F32R)
        pT_lo = sb("pT_lo", [P, 2, tokens], F32R)
        row_max = sb("row_max", [P, NT])
        neg_max = sb("neg_max", [P, NT])
        neg_max_fc = sb("neg_max_fc", [P, NT])
        neg_top_fc = sb("neg_top_fc", [P, NT])
        f2_max = sb("f2_max", [P, 1])
        den = sb("den", [P, NT])
        rden = sb("rden", [P, NT])
        neg_part = sb("neg_part", [P, 2, hid])
        pos_part = sb("pos_part", [P, 2, hid])
        stats = sb("stats", [P, NT, 6])
        spare = sb("spare", [P, NT])
        mv = sb("mv", [P, NT, 2])
        var_eps = sb("var_eps", [P, NT])
        rstd = sb("rstd", [P, NT])

        p_turn = pb("p_turn", [P, 2, tokens])
        acc = pb("acc", [P, 2, 512])
        proj = pb("proj", [P, 2, 512])

        s_load = sem("weights_loaded")
        s_adj = sem("adj_loaded")
        s_mask = sem("mask_built")
        s_wa = sem("weights_ready")
        s_wa_steps = sem("wa_steps")
        s_id0 = sem("ident_zeroed")
        s_id = sem("ident_ready")
        x_loaded = sem("x_loaded")
        x1_copied = sem("x1_copied")
        out_stored = sem("out_stored")
        masked_done = sem("masked_scores_done")
        w_done = sem("sloped_scores_done")
        leaky_done = sem("leaky_scores_done")
        fc_top_done = sem("fc_top_done")
        fc_max_done = sem("fc_max_done")
        z_done = sem("scores_done")
        g0_f_done = sem("graph_f_done")
        hand_f_done = sem("hand_f_done")
        p_done = sem("prob_done")
        t_done = sem("prob_turned")
        hi_done = sem("prob_hi_done")
        lo_done = sem("prob_lo_done")
        mm_done = sem("attention_summed")
        rd_done = sem("rden_done")
        acc_free = sem("acc_read")
        neg_done = sem("neg_part_done")
        e1_done = sem("first_exp_done")
        e2_done = sem("second_exp_done")
        elu_done = sem("elu_done")
        res_done = sem("residual_added")
        sum_done = sem("block_sum_done")
        bst_done = sem("bn_stats_done")
        stat_done = sem("mean_var_done")
        veps_done = sem("var_eps_done")
        rstd_done = sem("rstd_done")
        ln_done = sem("layer_norm_done")
        u_done = sem("unit_summed")
        u_hi = sem("unit_hi_done")
        u_lo = sem("unit_lo_done")
        u_free = [sem("bank0_read"), sem("bank1_read")]

        def evacuated(eng, at, n):
            for bank in u_free:
                wait(eng, bank, at.pairs + n // 2)

        block = ctx.enter_context(nc.Block())

        @block.sync
        def _(sp):
            vectors = [(a0, 0), (afc, 2 * feat), (ah, 2 * feat + 2 * hid)]
            flat_res = x1_res[:, :, :].rearrange("p t f -> p (t f)")
            sp.dma_start(x_nat[:, :, :], x[0].rearrange("(t p) f -> p t f", p=P)).then_inc(x_loaded, 16)
            sp.dma_start(w0e[:, :, 0:feat], w0.rearrange("(k p) n -> p k n", p=P)).then_inc(s_load, 16)
            for a, at in vectors:
                n = a.shape[0]
                sp.dma_start(flat_res[:, at:at + n], a.rearrange("n o -> (o n)").partition_broadcast(P)).then_inc(s_load, 16)
            adj_t = adj.rearrange("(t p) j -> p t j", p=P)
            sp.dma_start(rT[:, :, :].bitcast(I32), adj_t[:, 0:4, :]).then_inc(s_adj, 16)
            sp.dma_start(w1s[:, :, :], w1.rearrange("(k p) n -> p k n", p=P)).then_inc(s_load, 16)
            sp.dma_start(wfcs[:, :, :], wfc.rearrange("(k p) n -> p k n", p=P)).then_inc(s_load, 16)
            sp.dma_start(w2s[:, :, :], w2.rearrange("(k p) n -> p k n", p=P)).then_inc(s_load, 16)
            sp.dma_start(whe[:, :, 0:feat], wh.rearrange("(k p) n -> p k n", p=P)).then_inc(s_load, 16)
            with nc.allow_non_contiguous_dma(reason="768 bias values, once"):
                sp.dma_start(b1c[:, :], b1.rearrange("(k p) -> p k", p=P)).then_inc(s_load, 16)
                sp.dma_start(b2c[:, :], b2.rearrange("(k p) -> p k", p=P)).then_inc(s_load, 16)
            sp.wait_ge(s_mask, 1)
            sp.dma_start(rT[:, :, :].bitcast(I32), adj_t[:, 4:8, :]).then_inc(s_adj, 16)

            def phase(name, at, nxt):
                b = at.batch
                if name == "A":
                    sp.wait_ge(ln_done, at.masked)
                    sp.wait_ge(out_stored, 16 * (b + 1))
                    sp.dma_start(x1_res[:, :, :], x1[:, :, :]).then_inc(x1_copied, 16)
                if name == "B":
                    more = not isinstance(b, int) or b + 1 < batches
                    if more:
                        sp.wait_ge(acc_free, at.tile + NT)
                        sp.dma_start(x_nat[:, :, :], x[b + 1].rearrange("(t p) f -> p t f", p=P)
                                     if isinstance(b, int) else
                                     x[bass.ds(b + 1, 1)].rearrange("o (t p) f -> p (o t) f", p=P)).then_inc(x_loaded, 16)
                if name == "E":
                    sp.wait_ge(ln_done, at.masked + NT)
                    sp.dma_start(out[b].rearrange("(t p) f -> p t f", p=P) if isinstance(b, int) else
                                 out[bass.ds(b, 1)].rearrange("o (t p) f -> p (o t) f", p=P),
                                 x1_res[:, :, :]).then_inc(out_stored, 16)

            sp.sem_inc(out_stored, 16)
            walk(sp, batches, phase, lambda name, at: None)
            sp.wait_ge(out_stored, 16 * (batches + 1))

        @block.gpsimd
        def _(pool):
            pool.memset(half_neg[:, :], -0.5)
            pool.memset(eps[:, :], EPS)
            pool.memset(ident[:, :], 0.0).then_inc(s_id0, 1)
            pool.wait_ge(s_id0, 1)
            pool.affine_select(out=ident[:, :], in_=ident[:, :], compare_op=ALU.not_equal, fill=1.0, base=0,
                               pattern=[[-1, P]], channel_multiplier=1).then_inc(s_id, 1)
            pool.wait_ge(s_id, 1)

            def phase(name, at, nxt):
                if name not in "BE":
                    return
                for t in range(NT):
                    pool.wait_ge(stat_done, at.masked + t + 1)
                    pool.tensor_tensor(var_eps[:, t:t + 1], mv[:, t, 1:2], eps[:, :], ALU.add).then_inc(veps_done, 1)
                    pool.wait_ge(veps_done, at.masked + t + 1)
                    pool.tensor_tensor(rstd[:, t:t + 1], var_eps[:, t:t + 1], half_neg[:, :], ALU.pow).then_inc(rstd_done, 1)

            walk(pool, batches, phase, lambda name, at: None)

        @block.scalar
        def _(act):
            def sloped_tile(name, at, t):
                layer = LAYER[name]
                if t == 0:
                    f_ready(name, at)
                wait(act, p_done, at.tile + t - 1)
                act.activation(zbuf[:, t % 2, :], f2b[:, layer, :], ACT.Identity, bias=fcol[:, layer, t, 2:3],
                               scale=SLOPE).then_inc(w_done, 1)

            def f_ready(name, at):
                wait(act, {"A": fc_max_done, "B": g0_f_done, "E": hand_f_done}[name],
                     {"A": at.fc, "B": at.g0, "E": at.hand}[name])

            def prob_tile(name, at, t):
                slot, top = t % 2, neg_max_fc if name == "A" else neg_max
                act.wait_ge(z_done, at.tile + t + 1)
                wait(act, t_done, at.tile + t - 1)
                act.activation(prob[:, slot, :], zbuf[:, slot, :], ACT.Exp, bias=top[:, t:t + 1],
                               accum_out=den[:, t:t + 1]).then_inc(p_done, 1)

            def turned_hi(at, t):
                act.wait_ge(t_done, at.tile + t + 1)
                wait(act, mm_done, at.tile + t - 1)
                act.activation(pT_hi[:, t % 2, :], p_turn[:, t % 2, :], ACT.Copy).then_inc(hi_done, 1)

            def elu_exps(name, at, t):
                part = neg_part[:, t % 2, 0:WIDTH[name]]
                act.wait_ge(neg_done, at.elu + t + 1)
                act.activation(part, part, ACT.Exp).then_inc(e1_done, 1)
                act.wait_ge(e1_done, at.elu + t + 1)
                act.activation(part, part, ACT.Exp, bias=minus_one[:, :]).then_inc(e2_done, 1)

            def attention(name, at, nxt):
                after = At(add(at.counts, name), 0)
                for t in range(NT + 1):
                    if t < NT:
                        turned_hi(at, t)
                        if t + 2 < NT:
                            sloped_tile(name, at, t + 2)
                        elif nxt:
                            sloped_tile(nxt, after, t + 2 - NT)
                        if t + 1 < NT:
                            prob_tile(name, at, t + 1)
                        elif nxt:
                            prob_tile(nxt, after, 0)
                    if t >= 1 and name != "B":
                        elu_exps(name, at, t - 1)

            def unit(at, n, dst, func=ACT.Copy, width=512, last=True, **more):
                act.wait_ge(u_done, at.unit + n + 1)
                ins = act.activation(dst, proj[:, n % 2, 0:width], func, **more)
                ins.then_inc(u_free[n % 2] if last else u_hi, 1)

            def transposed_in(at):
                for n in range(0, 4, 2):
                    unit(at, n, xT[:, n // 2, 0:HALF])

            def split_hi(at, n, h, t):
                unit(at, n, h[:, 0, t, :], width=h.shape[3], last=False)

            def phase(name, at, nxt):
                if name in "ABE":
                    attention(name, at, nxt)
                if name == "F":
                    transposed_in(at)
                    for t in range(NT):
                        split_hi(at, 4 + t, h_slim, t)
                    unit(at, 12, f2b[:, G0, 0:HALF])
                if name == "C":
                    for m in range(KF):
                        unit(at, 2 * m, xT[:, m, 0:HALF], ACT.Relu, bias=b2c[:, m:m + 1])
                    for t in range(NT):
                        split_hi(at, 4 + t, h_slim, t)
                    unit(at, 12, f2b[:, HAND, 0:HALF])
                    for j in range(0, 4, 2):
                        unit(at, 14 + j, o_nat[:, 2 * j:2 * j + 2, :].rearrange("p t f -> p (t f)"))
                if name == "D":
                    transposed_in(at)
                    for m in range(KH):
                        unit(at, 4 + 2 * m, rT[:, m, 0:HALF], ACT.Relu, bias=b1c[:, m:m + 1])
                    for t in range(NT):
                        split_hi(at, 12 + t, h_wide, t)
                    unit(at, 22, f2b[:, FC, 0:HALF])

            act.wait_ge(s_wa, 1)
            

            def ahead(name, at):
                sloped_tile(name, at, 0)
                sloped_tile(name, at, 1)
                prob_tile(name, at, 0)

            walk(act, batches, phase, ahead)

        @block.tensor
        def _(pe):
            def turn_prob(at, t):
                slot = t % 2
                pe.wait_ge(p_done, at.tile + t + 1)
                wait(pe, lo_done, at.tile + t - 1)
                for j in range(NT):
                    ins = pe.transpose(p_turn[:, slot, j * P:(j + 1) * P], prob[:, slot, j * P:(j + 1) * P], ident[:, :])
                ins.then_inc(t_done, 1)

            def weigh(name, at, t):
                slot, h, w = t % 2, H[name], WIDTH[name]
                pe.wait_ge(lo_done, at.tile + t + 1)
                wait(pe, acc_free, at.tile + t - 1)
                to = acc[:, slot, 0:w]
                for j in range(NT):
                    hi, lo = pT_hi[:, slot, j * P:(j + 1) * P], pT_lo[:, slot, j * P:(j + 1) * P]
                    pe.matmul(to, hi, h[:, 0, j, :], start=(j == 0), stop=False)
                    pe.matmul(to, hi, h[:, 1, j, :], start=False, stop=False)
                    ins = pe.matmul(to, lo, h[:, 0, j, :], start=False, stop=(j == NT - 1))
                ins.then_inc(mm_done, 1)

            def unit(at, n, steps):
                wait(pe, u_free[n % 2], at.pairs + n // 2)
                for cols, left, right, start, stop in steps:
                    to = proj[:, n % 2, cols[0]:cols[1]]
                    if left is None:
                        ins = pe.transpose(to, right, ident[:, :])
                    else:
                        ins = pe.matmul(to, left, right, start=start, stop=stop)
                ins.then_inc(u_done, 1)

            def turned(blocks):
                return [((i * P, (i + 1) * P), None, b, True, True) for i, b in enumerate(blocks)]

            def summed(width, pairs, at=0):
                return [((at, at + width), l, r, i == 0, i == len(pairs) - 1) for i, (l, r) in enumerate(pairs)]

            def turn_in(at, src):
                for n in range(4):
                    c, first = n // 2, 4 * (n % 2)
                    unit(at, n, turned([src[:, first + j, c * P:(c + 1) * P] for j in range(4)]))
                evacuated(pe, at, 4)

            def spread_f2(at, n, layer):
                evacuated(pe, at, n)
                for half in range(2):
                    unit(at, n + half, turned([fcol[:, layer, 4 * half + j, 1:2].to_broadcast([P, P]) for j in range(4)]))

            def project(at, n, weights, src, width, k):
                for t in range(NT):
                    unit(at, n + t, summed(width, [(src[:, c, t * P:(t + 1) * P], weights[:, c, 0:width]) for c in range(k)]))

            def elu_turned(at, t):
                pe.wait_ge(elu_done, at.elu + t + 1)
                unit(at, t, turned([pos_part[:, t % 2, m * P:(m + 1) * P] for m in range(KH)]))

            def phase(name, at, nxt):
                if name in "ABE":
                    first = isinstance(at.batch, int) and at.batch == 0
                    evacuated(pe, at, 0 if name != "B" or first else -ADDS["A"]["unit"])
                    for t in range(NT):
                        if t + 1 < NT:
                            turn_prob(at, t + 1)
                        elif nxt:
                            turn_prob(At(add(at.counts, name), 0), 0)
                        weigh(name, at, t)
                        if name == "A" and t >= 2:
                            elu_turned(at, t - 2)
                    if name == "A":
                        elu_turned(at, NT - 2)
                        elu_turned(at, NT - 1)
                if name == "F":
                    pe.wait_ge(x_loaded, 16 * (at.batch + 1))
                    turn_in(at, x_nat)
                    project(at, 4, w0e, xT, feat + 3, KF)
                    spread_f2(at, 12, G0)
                if name == "C":
                    evacuated(pe, at, 0)
                    for n in range(4):
                        m, half = n // 2, n % 2
                        unit(at, n, summed(HALF, [(w2s[:, c, m * P:(m + 1) * P], rT[:, c, half * HALF:(half + 1) * HALF])
                                                  for c in range(KH)]))
                    evacuated(pe, at, 4)
                    project(at, 4, whe, xT, feat + 3, KF)
                    spread_f2(at, 12, HAND)
                    for j in range(4):
                        unit(at, 14 + j, turned([xT[:, c, t * P:(t + 1) * P] for t in (2 * j, 2 * j + 1) for c in range(KF)]))
                if name == "D":
                    pe.wait_ge(ln_done, at.masked)
                    turn_in(at, x1)
                    for n in range(8):
                        m, half = n // 2, n % 2
                        unit(at, 4 + n, summed(HALF, [(w1s[:, c, m * P:(m + 1) * P], xT[:, c, half * HALF:(half + 1) * HALF])
                                                      for c in range(KF)]))
                    evacuated(pe, at, 12)
                    project(at, 12, wfcs, rT, hid, KH)
                    for half in range(2):
                        steps = []
                        for j in range(4):
                            t = 4 * half + j
                            steps += summed(3, [(rT[:, c, t * P:(t + 1) * P], wfa[:, c, :]) for c in range(KH)], at=3 * j)
                        unit(at, 20 + half, steps)
                    spread_f2(at, 22, FC)

            pe.wait_ge(s_id, 1)
            pe.wait_ge(s_wa, 1)
            walk(pe, batches, phase, lambda name, at: turn_prob(at, 0))

        @block.vector
        def _(dve):
            dve.wait_ge(s_load, 16 * 10)
            flat_res = x1_res[:, :, :].rearrange("p t f -> p (t f)")
            n = 0
            for w, cols, a_at, fan, k in ((w0e, w0e[:, :, feat:], 0, feat, KF), (wfcs, wfa, 2 * feat, hid, KH),
                                          (whe, whe[:, :, feat:], 2 * feat + 2 * hid, feat, KF)):
                for c in range(k):
                    for part in range(2):
                        wait(dve, s_wa_steps, n)
                        dve.tensor_tensor_reduce(neg_part[:, 0, 0:fan], w[:, c, 0:fan],
                                                 flat_res[:, a_at + part * fan:a_at + (part + 1) * fan], 1.0, 0.0,
                                                 ALU.mult, ALU.add, cols[:, c, part:part + 1]).then_inc(s_wa_steps, 1)
                        n += 1
            dve.wait_ge(s_wa_steps, n)
            for cols in (w0e[:, :, feat:], wfa, whe[:, :, feat:]):
                dve.tensor_scalar(cols[:, :, 2:3], cols[:, :, 0:1], SLOPE, None, ALU.mult).then_inc(s_wa_steps, 1)
            dve.wait_ge(s_wa_steps, n + 3)
            for half in range(2):
                dve.wait_ge(s_adj, 16 * (half + 1))
                dve.tensor_scalar(mask_add[:, 4 * half:4 * half + 4, :], rT[:, :, :].bitcast(I32), 0.0, MASKED,
                                  ALU.is_le, ALU.mult).then_inc(s_mask, 1)
            dve.wait_ge(s_mask, 2)
            dve.memset(minus_one[:, :], -1.0).then_inc(s_wa, 1)

            def score_tile(name, at, t):
                layer, z = LAYER[name], zbuf[:, t % 2, :]
                dve.wait_ge(w_done, at.tile + t + 1)
                ins = dve.scalar_tensor_tensor(out=z, in0=f2b[:, layer, :], scalar=fcol[:, layer, t, 0:1], in1=z,
                                               op0=ALU.add, op1=ALU.max)
                if name == "A":
                    ins.then_inc(z_done, 1)
                    return
                ins.then_inc(leaky_done, 1)
                dve.wait_ge(leaky_done, at.masked + t + 1)
                dve.tensor_copy(spare[:, t:t + 1], fcol[:, layer, t, 0:1])
                dve.tensor_tensor_reduce(z, z, mask_add[:, t, :], 1.0, LOWEST, ALU.add, ALU.max,
                                         row_max[:, t:t + 1]).then_inc(masked_done, 1)
                dve.wait_ge(masked_done, at.masked + t + 1)
                dve.tensor_scalar(neg_max[:, t:t + 1], row_max[:, t:t + 1], -1.0, None, ALU.mult).then_inc(z_done, 1)

            def turned_lo(at, t):
                dve.wait_ge(hi_done, at.tile + t + 1)
                dve.tensor_tensor(pT_lo[:, t % 2, :], p_turn[:, t % 2, :], pT_hi[:, t % 2, :].bitcast(F32),
                                  ALU.subtract).then_inc(lo_done, 1)

            def row_scale(at, t):
                dve.wait_ge(mm_done, at.tile + t + 1)
                dve.reciprocal(rden[:, t:t + 1], den[:, t:t + 1]).then_inc(rd_done, 1)
                dve.wait_ge(rd_done, at.tile + t + 1)

            def elu_parts(name, at, t):
                w = WIDTH[name]
                row_scale(at, t)
                if t >= 2:
                    dve.wait_ge(elu_done, at.elu + t - 1)
                dve.tensor_scalar(neg_part[:, t % 2, 0:w], acc[:, t % 2, 0:w], rden[:, t:t + 1], 0.0,
                                  ALU.mult, ALU.min).then_inc(neg_done, 1)
                if t >= 2:
                    if name == "A":
                        dve.wait_ge(u_done, at.unit + t - 1)
                    else:
                        dve.wait_ge(res_done, at.resid + t - 1)
                dve.tensor_scalar(pos_part[:, t % 2, 0:w], acc[:, t % 2, 0:w], rden[:, t:t + 1], 0.0,
                                  ALU.mult, ALU.max).then_inc(acc_free, 1)

            def elu_sum(name, at, t):
                w = WIDTH[name]
                dve.wait_ge(e2_done, at.elu + t + 1)
                dve.wait_ge(acc_free, at.tile + t + 1)
                dve.scalar_tensor_tensor(out=pos_part[:, t % 2, 0:w], in0=neg_part[:, t % 2, 0:w], scalar=-1.0,
                                         in1=pos_part[:, t % 2, 0:w], op0=ALU.add, op1=ALU.add).then_inc(elu_done, 1)

            def add_r(at, t):
                dve.wait_ge(u_done, at.unit + t + 1)
                cols = rT[:, :, t * P:(t + 1) * P]
                dve.tensor_tensor(cols, proj[:, t % 2, :].rearrange("p (m i) -> p m i", m=KH), cols,
                                  ALU.add).then_inc(u_free[t % 2], 1)

            def mean_var(at, t, y):
                dve.bn_stats(stats[:, t, :], y).then_inc(bst_done, 1)
                dve.wait_ge(bst_done, at.masked + t + 1)
                dve.tensor_copy(spare[:, t:t + 1], stats[:, t, 0:1])
                dve.bn_aggr(mv[:, t, :], stats[:, t, :]).then_inc(stat_done, 1)

            def normed(at, t, y):
                dve.wait_ge(rstd_done, at.masked + t + 1)
                dve.tensor_scalar(y, y, mv[:, t, 0:1], rstd[:, t:t + 1], ALU.subtract, ALU.mult).then_inc(ln_done, 1)

            def add_x(at, t):
                row_scale(at, t)
                if t == 0:
                    wait(dve, x1_copied, 16 * at.batch)
                dve.scalar_tensor_tensor(out=x1[:, t, :], in0=acc[:, t % 2, 0:feat], scalar=rden[:, t:t + 1],
                                         in1=x_nat[:, t, :], op0=ALU.mult, op1=ALU.add).then_inc(acc_free, 1)
                dve.wait_ge(acc_free, at.tile + t + 1)
                mean_var(at, t, x1[:, t, :])

            def block_out(at, t):
                elu_sum("E", at, t)
                dve.wait_ge(elu_done, at.elu + t + 1)
                g = pos_part[:, t % 2, 0:feat]
                dve.tensor_tensor(g, g, o_nat[:, t, :], ALU.add).then_inc(res_done, 1)
                dve.wait_ge(res_done, at.resid + t + 1)
                if t == 0:
                    dve.wait_ge(x1_copied, 16 * (at.batch + 1))
                dve.scalar_tensor_tensor(out=x1_res[:, t, :], in0=g, scalar=0.0, in1=x1_res[:, t, :],
                                         op0=ALU.max, op1=ALU.add).then_inc(sum_done, 1)
                dve.wait_ge(sum_done, at.resid + t + 1)
                mean_var(at, t, x1_res[:, t, :])

            def attention(name, at, nxt):
                for t in range(NT + 3):
                    if t < NT:
                        turned_lo(at, t)
                        if t + 2 < NT:
                            score_tile(name, at, t + 2)
                        elif nxt:
                            score_tile(nxt, At(add(at.counts, name), 0), t + 2 - NT)
                    if name == "B":
                        if 1 <= t <= NT:
                            add_x(at, t - 1)
                        if 2 <= t <= NT + 1:
                            normed(at, t - 2, x1[:, t - 2, :])
                    else:
                        if 1 <= t <= NT:
                            elu_parts(name, at, t - 1)
                        if 2 <= t <= NT + 1:
                            if name == "A":
                                elu_sum(name, at, t - 2)
                            else:
                                block_out(at, t - 2)
                        if t >= 3:
                            if name == "A":
                                add_r(at, t - 3)
                            else:
                                normed(at, t - 3, x1_res[:, t - 3, :])

            def unit(at, n, dst, src=None):
                dve.wait_ge(u_done, at.unit + n + 1)
                dve.tensor_copy(dst, proj[:, n % 2, :] if src is None else src).then_inc(u_free[n % 2], 1)

            def relu_unit(at, n, dst, bias):
                dve.wait_ge(u_done, at.unit + n + 1)
                dve.tensor_scalar(dst, proj[:, n % 2, :], bias, 0.0, ALU.add, ALU.max).then_inc(u_free[n % 2], 1)

            def split_lo(at, n, h, t, layer=None):
                w = h.shape[3]
                dve.wait_ge(u_hi, at.split + t + 1)
                ins = dve.tensor_tensor(h[:, 1, t, :], proj[:, n % 2, 0:w], h[:, 0, t, :].bitcast(F32), ALU.subtract)
                if layer is not None:
                    ins = dve.tensor_copy(fcol[:, layer, t, :], proj[:, n % 2, w:w + 3])
                ins.then_inc(u_free[n % 2], 1)

            def f_whole(at, n, done):
                evacuated(dve, at, n)
                dve.tensor_copy(spare[:, 0:1], f2b[:, 0, 0:1]).then_inc(done, 1)

            def transposed_in(at):
                for n in range(1, 4, 2):
                    unit(at, n, xT[:, n // 2, HALF:tokens])

            def phase(name, at, nxt):
                if name in "ABE":
                    attention(name, at, nxt)
                if name == "F":
                    transposed_in(at)
                    for t in range(NT):
                        split_lo(at, 4 + t, h_slim, t, G0)
                    unit(at, 13, f2b[:, G0, HALF:tokens])
                    f_whole(at, 14, g0_f_done)
                if name == "C":
                    for m in range(KF):
                        relu_unit(at, 2 * m + 1, xT[:, m, HALF:tokens], b2c[:, m:m + 1])
                    for t in range(NT):
                        split_lo(at, 4 + t, h_slim, t, HAND)
                    unit(at, 13, f2b[:, HAND, HALF:tokens])
                    f_whole(at, 14, hand_f_done)
                    for j in range(1, 4, 2):
                        unit(at, 14 + j, o_nat[:, 2 * j:2 * j + 2, :].rearrange("p t f -> p (t f)"))
                if name == "D":
                    transposed_in(at)
                    for m in range(KH):
                        relu_unit(at, 5 + 2 * m, rT[:, m, HALF:tokens], b1c[:, m:m + 1])
                    for t in range(NT):
                        split_lo(at, 12 + t, h_wide, t)
                    for half in range(2):
                        unit(at, 20 + half, fcol[:, FC, 4 * half:4 * half + 4, :].rearrange("p t c -> p (t c)"),
                             proj[:, half, 0:12])
                    unit(at, 23, f2b[:, FC, HALF:tokens])
                    evacuated(dve, at, 24)
                    dve.tensor_reduce(f2_max[:, :], f2b[:, FC, :], AX.X, ALU.max).then_inc(fc_top_done, 1)
                    dve.wait_ge(fc_top_done, 2 * at.fc + 1)
                    dve.tensor_scalar(neg_top_fc[:, :], fcol[:, FC, :, 0], f2_max[:, 0:1], -1.0,
                                      ALU.add, ALU.mult).then_inc(fc_top_done, 1)
                    dve.wait_ge(fc_top_done, 2 * at.fc + 2)
                    dve.scalar_tensor_tensor(out=neg_max_fc[:, :], in0=neg_top_fc[:, :], scalar=SLOPE,
                                             in1=neg_top_fc[:, :], op0=ALU.mult, op1=ALU.min).then_inc(fc_max_done, 1)

            def ahead(name, at):
                score_tile(name, at, 0)
                score_tile(name, at, 1)

            walk(dve, batches, phase, ahead)


def kernel(**inputs):
    import numpy as np
    import concourse.bacc as bacc
    from concourse.bass_utils import run_bass_kernel_spmd

    order = ["x", "adj", "L0_gnn_W", "L0_gnn_a", "L1_gnn_mlp1_w", "L1_gnn_mlp1_b", "L1_gnn_mlp2_w", "L1_gnn_mlp2_b",
             "L1_gnn_W_fc", "L1_gnn_a_fc", "L1_gnn_W_hand", "L1_gnn_a_hand"]
    nc = bacc.Bacc("TRN2", target_bir_lowering=False, num_devices=1)
    arrays, args = {}, []
    for name in order:
        a = np.ascontiguousarray(inputs[name])
        arrays[f"in_{name}"] = a
        args.append(nc.dram_tensor(f"in_{name}", a.shape, mybir.dt.from_np(a.dtype), kind="ExternalInput").ap())
    out = nc.dram_tensor("out_x", arrays["in_x"].shape, F32, kind="ExternalOutput").ap()
    build(nc, *args, out)
    return run_bass_kernel_spmd(nc, [arrays], core_ids=[0]).results[0]["out_x"]
```

```python
from contextlib import ExitStack

import concourse.bass as bass
import concourse.mybir as mybir

F32 = mybir.dt.float32
F32R = mybir.dt.float32r
BF16 = mybir.dt.bfloat16
I32 = mybir.dt.int32
ACT = mybir.ActivationFunctionType
ALU = mybir.AluOpType
AX = mybir.AxisListType

P = 128
SLOPE = 0.2
MASKED = -9e15
EPS = 1e-5
LOWEST = -3.0e38

TILES = 8


def units(side, text):
    return [[(w[0], w[1], int(w[2:])) for w in (v if v[0].isupper() else side + v for v in step.split())]
            for step in text.split("|")]


PLAN = {
    "F": (None, units("F", "x0 x1 x2 x3|h0 h1 h2 h3 h4 h5 h6 h7|r0 r1")),
    "B": ("B", units("B", "|||||||")),
    "D": (None, units("D", "||x0 x1 x2 x3|m0 m1 m2 m3 m4 m5 m6 m7|h0 h1 h2 h3 h4 h5 h6 h7|r0 r1|"
                           "i0 i1 i2 i3 i4 i5 i6 i7")),
    "AF": ("A", units("F", "|x0 x1 x2 x3|h0 h1 h2 g0|h3 h4 h5 g1|h6 h7 r0 g2 r1|g3|g4|g5")),
    "BC": ("B", units("C", "m0 g6|m1 g7|h0 h1 h2 m2|h3 m3|h4 h5 h6 h7 r0 o0 o1 r1|o2 o3|Dx0 Dx1 Dm0 Dm1|Dm2 Dm3")),
    "ED": ("E", units("D", "h0 h1 h2|h3 i0|x2 x3 i1 m4 m5|m6 m7 i2 h4|h5 h6 h7 r0 i3 r1|i4 i5|i6 i7|")),
    "A": ("A", units("F", "||g0|g1|g2|g3|g4|g5")),
    "C": (None, units("C", "g6|g7|m0 m1|m2 m3|h0 h1 h2 h3 h4 h5 h6 h7|r0 r1|o0 o1 o2 o3")),
    "E": ("E", units("E", "|||||||")),
    "end": (None, units("E", "||")),
}
ORDER = {p: [u for step in steps for u in step] for p, (_, steps) in PLAN.items()}
FIRST = ["F", "ahead B", "B", "D", "ahead A"]
BODY = ["AF", "BC", "ED"]
LAST = ["A", "C", "ahead E", "E", "end"]
NEXT = {"AF": "B", "BC": "E", "ED": "A"}


def adds(p):
    att, n = PLAN[p][0], len(ORDER[p])
    assert n % 2 == 0
    return dict(tile=TILES * (att is not None), masked=TILES * (att in ("B", "E")), elu=TILES * (att in ("A", "E")),
                resid=TILES * (att == "E"), unit=n, pairs=n // 2, split=sum(k in "hi" for _, k, _ in ORDER[p]),
                f_graph=ORDER[p].count(("F", "r", 1)), f_hand=ORDER[p].count(("C", "r", 1)),
                f_full=ORDER[p].count(("D", "r", 1)))


NAMES = list(adds("F"))


def add(counts, phases):
    return {n: counts[n] + sum(adds(p)[n] for p in phases) for n in NAMES}


class At:

    def __init__(self, p, counts, batch, prev=None):
        self.p, self.counts, self.batch, self.prev = p, counts, batch, prev

    def __getattr__(self, name):
        return self.counts[name]

    def after(self):
        return At(None, add(self.counts, [self.p]), self.batch, self)

    def index(self, kind, n, side=None):
        return next(i for i, u in enumerate(ORDER[self.p]) if u[1:] == (kind, n) and side in (None, u[0]))

    def made(self, kind, n, side):
        return next((i + 1 for i, u in enumerate(ORDER[self.p]) if u == (side, kind, n)), 0)

    def splits(self, n):
        return sum(u[1] in "hi" for u in ORDER[self.p][:n])

    def whole_h(self):
        return max(i + 1 for i, u in enumerate(ORDER[self.p]) if u[1] in "hi")


def walk(eng, batches, phase, ahead):

    def run(counts, k, items, prev):
        done = []
        for item in items:
            at = At(item, add(counts, done), k, prev)
            if item.startswith("ahead"):
                ahead(item[-1], at)
            else:
                phase(at, NEXT.get(item))
                done.append(item)
                prev = at

    zero = {n: 0 for n in NAMES}
    start = add(zero, ["F", "B", "D"])
    per = add(zero, BODY)

    def begin(k):
        return {n: k * per[n] + start[n] for n in NAMES}

    def begin_last(k):
        return {n: k * per[n] + (start[n] - adds("ED")[n]) for n in NAMES}

    run(zero, -1, FIRST, None)
    run(start, 0, BODY, At("D", add(zero, ["F", "B"]), -1))
    with eng.Fori(1, batches - 1) as k:
        run(begin(k), k, BODY, At("ED", begin_last(k), k - 1))
    k = batches - 1
    run(begin(k), k, LAST, At("ED", begin_last(k), k - 1))


def steps_of(at):
    att, steps = PLAN[at.p]
    n = 0
    for s, step in enumerate(steps):
        yield s, att, [(n + i, *u) for i, u in enumerate(step)]
        n += len(step)


def at_distance(at, s, nxt=None):
    att = PLAN[at.p][0]
    if 0 <= s < TILES and att:
        return att, at, s
    if s < 0 and at.prev and PLAN[at.prev.p][0]:
        return PLAN[at.prev.p][0], at.prev, s + TILES
    if s >= TILES and nxt:
        return nxt, at.after(), s - TILES
    return None


def wait(eng, sem, value):
    if isinstance(value, int) and value <= 0:
        return
    eng.wait_ge(sem, value)


def build(nc, x, adj, w0, a0, w1, b1, w2, b2, wfc, afc, wh, ah, out):
    batches, tokens, feat = x.shape
    hid = w1.shape[1]
    NT = tokens // P
    KF = feat // P
    KH = hid // P
    HALF = tokens // 2
    assert (NT, KF, KH, HALF) == (8, 2, 4, 512)
    G0, FC, HAND = 0, 1, 2
    LAYER = {"A": FC, "B": G0, "E": HAND}
    F_OF = {"D": FC, "F": G0, "C": HAND}
    WIDTH = {"A": hid, "B": feat, "E": feat}

    ctx = ExitStack()
    with ctx:
        def sb(name, shape, dt=F32):
            return ctx.enter_context(nc.sbuf_tensor(name, shape, dt))

        def pb(name, shape):
            return ctx.enter_context(nc.psum_tensor(name, shape, F32))

        def sem(name):
            return ctx.enter_context(nc.semaphore(name))

        w0e = sb("w0e", [P, KF, feat + 3])
        w1s = sb("w1s", [P, KF, hid])
        wfce = sb("wfce", [P, KH, hid + 3])
        w2s = sb("w2s", [P, KH, feat])
        whe = sb("whe", [P, KF, feat + 3])
        b1c = sb("b1c", [P, KH])
        b2c = sb("b2c", [P, KF])
        ident = sb("ident", [P, P])
        minus_half = sb("minus_half", [P, 1])
        eps = sb("eps", [P, 1])
        minus_one = sb("minus_one", [P, 1])
        mask_add = sb("mask_add", [P, NT, tokens], BF16)
        x_nat = sb("x_nat", [P, NT, feat])
        x1 = sb("x1", [P, NT, feat])
        x1_res = sb("x1_res", [P, NT, feat])
        o_nat = sb("o_nat", [P, NT, feat])
        h_wide = sb("h_wide", [P, 2, NT, hid], F32R)
        h_graph = sb("h_graph", [P, 2, NT, feat], F32R)
        h_hand = sb("h_hand", [P, 2, NT, feat], F32R)
        H = {"A": h_wide, "B": h_graph, "E": h_hand}
        H_OF = {"D": h_wide, "F": h_graph, "C": h_hand}
        xT = sb("xT", [P, KF, tokens])
        rT = sb("rT", [P, KH, tokens])
        fcol = sb("fcol", [P, 3, NT, 3])
        f2b = sb("f2b", [P, 3, tokens])
        zbuf = sb("zbuf", [P, 2, tokens])
        pT_hi = sb("pT_hi", [P, 2, tokens], F32R)
        pT_lo = sb("pT_lo", [P, 2, tokens], F32R)
        row_max = sb("row_max", [P, NT])
        neg_max = sb("neg_max", [P, NT])
        neg_max_fc = sb("neg_max_fc", [P, NT])
        neg_top_fc = sb("neg_top_fc", [P, NT])
        f2_max = sb("f2_max", [P, 1])
        den = sb("den", [P, NT])
        rden = sb("rden", [P, NT])
        neg_part = sb("neg_part", [P, 2, hid])
        pos_part = sb("pos_part", [P, 2, hid])
        stats = sb("stats", [P, NT, 6])
        spare = sb("spare", [P, NT])
        mv = sb("mv", [P, NT, 2])
        var_eps = sb("var_eps", [P, NT])
        rstd = sb("rstd", [P, NT])

        p_turn = pb("p_turn", [P, 2, tokens])
        acc = pb("acc", [P, 2, 512])
        proj = pb("proj", [P, 2, 512])

        s_load = sem("weights_loaded")
        s_adj = sem("adj_loaded")
        s_mask = sem("mask_built")
        s_wa = sem("weights_ready")
        s_wa_steps = sem("wa_steps")
        s_id0 = sem("ident_zeroed")
        s_id = sem("ident_ready")
        x_loaded = sem("x_loaded")
        x1_copied = sem("x1_copied")
        out_stored = sem("out_stored")
        masked_done = sem("masked_scores_done")
        w_done = sem("sloped_scores_done")
        leaky_done = sem("leaky_scores_done")
        fc_top_done = sem("fc_top_done")
        full_f_done = sem("full_f_done")
        z_done = sem("scores_done")
        graph_f_done = sem("graph_f_done")
        hand_f_done = sem("hand_f_done")
        p_done = sem("prob_done")
        t_done = sem("prob_turned")
        hi_done = sem("prob_hi_done")
        lo_done = sem("prob_lo_done")
        mm_done = sem("attention_summed")
        rd_done = sem("rden_done")
        acc_free = sem("acc_read")
        neg_done = sem("neg_part_done")
        e1_done = sem("first_exp_done")
        e2_done = sem("second_exp_done")
        elu_done = sem("elu_done")
        res_done = sem("residual_added")
        sum_done = sem("block_sum_done")
        bst_done = sem("bn_stats_done")
        stat_done = sem("mean_var_done")
        veps_done = sem("var_eps_done")
        rstd_done = sem("rstd_done")
        ln_done = sem("layer_norm_done")
        u_done = sem("unit_summed")
        u_hi = sem("unit_hi_done")
        u_lo = sem("unit_lo_done")
        u_free = [sem("bank0_read"), sem("bank1_read")]

        def block_place(side, j):
            return (rT, b1c, j % KH, j // KH) if side == "D" else (xT, b2c, j % KF, j // KF)

        def h_cols(side, kind, more=0):
            if side == "D":
                return slice(0, feat) if kind == "i" else slice(feat, hid + more)
            return slice(0, feat + more)

        def by_scalar(at, n):
            return n % 2 == 0 or at.p in ("BC", "ED")

        def evacuated(eng, at, n):
            wait(eng, u_free[0], at.pairs + (n + 1) // 2)
            wait(eng, u_free[1], at.pairs + n // 2)

        block = ctx.enter_context(nc.Block())

        @block.sync
        def _(sp):
            vectors = [(a0, 0), (afc, 2 * feat), (ah, 2 * feat + 2 * hid)]
            flat_res = x1_res[:, :, :].rearrange("p t f -> p (t f)")
            sp.dma_start(x_nat[:, :, :], x[0].rearrange("(t p) f -> p t f", p=P)).then_inc(x_loaded, 16)
            sp.dma_start(w0e[:, :, 0:feat], w0.rearrange("(k p) n -> p k n", p=P)).then_inc(s_load, 16)
            for a, at in vectors:
                n = a.shape[0]
                sp.dma_start(flat_res[:, at:at + n], a.rearrange("n o -> (o n)").partition_broadcast(P)).then_inc(s_load, 16)
            adj_t = adj.rearrange("(t p) j -> p t j", p=P)
            sp.dma_start(rT[:, :, :].bitcast(I32), adj_t[:, 0:4, :]).then_inc(s_adj, 16)
            sp.dma_start(w1s[:, :, :], w1.rearrange("(k p) n -> p k n", p=P)).then_inc(s_load, 16)
            sp.dma_start(wfce[:, :, 0:hid], wfc.rearrange("(k p) n -> p k n", p=P)).then_inc(s_load, 16)
            sp.dma_start(w2s[:, :, :], w2.rearrange("(k p) n -> p k n", p=P)).then_inc(s_load, 16)
            sp.dma_start(whe[:, :, 0:feat], wh.rearrange("(k p) n -> p k n", p=P)).then_inc(s_load, 16)
            with nc.allow_non_contiguous_dma(reason="768 bias values, once"):
                sp.dma_start(b1c[:, :], b1.rearrange("(k p) -> p k", p=P)).then_inc(s_load, 16)
                sp.dma_start(b2c[:, :], b2.rearrange("(k p) -> p k", p=P)).then_inc(s_load, 16)
            sp.wait_ge(s_mask, 1)
            sp.dma_start(rT[:, :, :].bitcast(I32), adj_t[:, 4:8, :]).then_inc(s_adj, 16)

            def store(b, masked):
                sp.wait_ge(ln_done, masked)
                sp.dma_start(out[b].rearrange("(t p) f -> p t f", p=P) if isinstance(b, int) else
                             out[bass.ds(b, 1)].rearrange("o (t p) f -> p (o t) f", p=P),
                             x1_res[:, :, :]).then_inc(out_stored, 16)

            def phase(at, nxt):
                b = at.batch
                if at.p == "AF":
                    sp.wait_ge(acc_free, at.tile if isinstance(b, int) and b == 0 else at.tile - TILES)
                    sp.dma_start(x_nat[:, :, :], x[b + 1].rearrange("(t p) f -> p t f", p=P) if isinstance(b, int) else
                                 x[bass.ds(b + 1, 1)].rearrange("o (t p) f -> p (o t) f", p=P)).then_inc(x_loaded, 16)
                if at.p in ("AF", "A"):
                    if isinstance(b, int) and b == 0:
                        sp.wait_ge(ln_done, at.masked)
                    else:
                        store(b - 1, at.masked)
                        sp.wait_ge(out_stored, 16 * b)
                    sp.dma_start(x1_res[:, :, :], x1[:, :, :]).then_inc(x1_copied, 16)
                if at.p == "end":
                    store(b, at.masked)

            walk(sp, batches, phase, lambda name, at: None)
            sp.wait_ge(out_stored, 16 * batches)

        @block.gpsimd
        def _(pool):
            pool.memset(minus_half[:, :], -0.5)
            pool.memset(eps[:, :], EPS)
            pool.memset(ident[:, :], 0.0).then_inc(s_id0, 1)
            pool.wait_ge(s_id0, 1)
            pool.affine_select(out=ident[:, :], in_=ident[:, :], compare_op=ALU.not_equal, fill=1.0, base=0,
                               pattern=[[-1, P]], channel_multiplier=1).then_inc(s_id, 1)
            pool.wait_ge(s_id, 1)

            def residual(at, t):
                pool.wait_ge(acc_free, at.tile + t + 1)
                g = pos_part[:, t % 2, 0:feat]
                pool.tensor_tensor(g, g, o_nat[:, t, :], ALU.add).then_inc(res_done, 1)

            def inverse_deviation(at, t):
                pool.wait_ge(stat_done, at.masked + t + 1)
                pool.tensor_tensor(var_eps[:, t:t + 1], mv[:, t, 1:2], eps[:, :], ALU.add).then_inc(veps_done, 1)
                pool.wait_ge(veps_done, at.masked + t + 1)
                pool.tensor_tensor(rstd[:, t:t + 1], var_eps[:, t:t + 1], minus_half[:, :], ALU.pow).then_inc(rstd_done, 1)

            def phase(at, nxt):
                if PLAN[at.p][0] == "B":
                    for t in range(NT):
                        inverse_deviation(at, t)
                elif PLAN[at.p][0] == "E":
                    for t in range(NT + 1):
                        if t < NT:
                            residual(at, t)
                        if t > 0:
                            inverse_deviation(at, t - 1)

            walk(pool, batches, phase, lambda name, at: None)

        @block.scalar
        def _(act):
            def sloped_tile(name, at, t):
                layer = LAYER[name]
                if t == 0:
                    f_ready(name, at)
                wait(act, t_done, at.tile + t - 1)
                act.activation(zbuf[:, t % 2, :], f2b[:, layer, :], ACT.Identity, bias=fcol[:, layer, t, 2:3],
                               scale=SLOPE).then_inc(w_done, 1)

            def f_ready(name, at):
                done, n = {"A": (full_f_done, at.f_full), "B": (graph_f_done, at.f_graph),
                           "E": (hand_f_done, at.f_hand)}[name]
                act.wait_ge(done, n)

            def prob_tile(name, at, t):
                slot, top = t % 2, neg_max_fc if name == "A" else neg_max
                act.wait_ge(z_done, at.tile + t + 1)
                act.activation(zbuf[:, slot, :], zbuf[:, slot, :], ACT.Exp, bias=top[:, t:t + 1],
                               accum_out=den[:, t:t + 1]).then_inc(p_done, 1)

            def turned_hi(name, at, t):
                act.wait_ge(t_done, at.tile + t + 1)
                wait(act, mm_done, at.tile + t - 1)
                act.activation(pT_hi[:, t % 2, :], p_turn[:, t % 2, :], ACT.Copy).then_inc(hi_done, 1)

            def elu_exps(name, at, t):
                part = neg_part[:, t % 2, 0:WIDTH[name]]
                act.wait_ge(neg_done, at.elu + t + 1)
                act.activation(part, part, ACT.Exp).then_inc(e1_done, 1)
                act.wait_ge(e1_done, at.elu + t + 1)
                act.activation(part, part, ACT.Exp, bias=minus_one[:, :]).then_inc(e2_done, 1)

            def unit(at, n, dst, func=ACT.Copy, width=512, last=True, **more):
                act.wait_ge(u_done, at.unit + n + 1)
                ins = act.activation(dst, proj[:, n % 2, 0:width], func, **more)
                ins.then_inc(u_free[n % 2] if last else u_hi, 1)

            def evacuate(at, n, side, kind, j):
                if kind in "hi":
                    h, cols = H_OF[side], h_cols(side, kind)
                    unit(at, n, h[:, 0, j, cols], width=feat, last=False)
                elif kind == "g" or not by_scalar(at, n):
                    return
                elif kind == "x":
                    unit(at, n, xT[:, j % 2, (j // 2) * HALF:(j // 2 + 1) * HALF])
                elif kind == "m":
                    dst, bias, m, half = block_place(side, j)
                    unit(at, n, dst[:, m, half * HALF:(half + 1) * HALF], ACT.Relu, bias=bias[:, m:m + 1])
                elif kind == "r":
                    unit(at, n, f2b[:, F_OF[side], j * HALF:(j + 1) * HALF])
                elif kind == "o":
                    unit(at, n, o_nat[:, 2 * j:2 * j + 2, :].rearrange("p t f -> p (t f)"))

            def phase(at, nxt):
                for s, att, work in steps_of(at):
                    ready, turned, later = (at_distance(at, s + d, nxt) if att else None for d in (2, 2, 4))
                    if ready:
                        prob_tile(*ready)
                    there = at_distance(at, s - 1)
                    if there and there[0] != "B":
                        elu_exps(*there)
                    if turned:
                        turned_hi(*turned)
                    for unit_of in work:
                        evacuate(at, *unit_of)
                    if later:
                        sloped_tile(*later)

            act.wait_ge(s_wa, 1)

            def ahead(name, at):
                sloped_tile(name, at, 0)
                sloped_tile(name, at, 1)
                for t in range(2):
                    prob_tile(name, at, t)
                for t in range(2):
                    turned_hi(name, at, t)
                sloped_tile(name, at, 2)
                sloped_tile(name, at, 3)

            walk(act, batches, phase, ahead)

        @block.tensor
        def _(pe):
            def turn_prob(name, at, t):
                slot = t % 2
                pe.wait_ge(p_done, at.tile + t + 1)
                wait(pe, lo_done, at.tile + t - 1)
                for j in range(NT):
                    ins = pe.transpose(p_turn[:, slot, j * P:(j + 1) * P], zbuf[:, slot, j * P:(j + 1) * P], ident[:, :])
                ins.then_inc(t_done, 1)

            def weigh(name, at, t):
                slot, h, w = t % 2, H[name], WIDTH[name]
                pe.wait_ge(lo_done, at.tile + t + 1)
                wait(pe, acc_free, at.tile + t - 1)
                to = acc[:, slot, 0:w]
                for j in range(NT):
                    hi, lo = pT_hi[:, slot, j * P:(j + 1) * P], pT_lo[:, slot, j * P:(j + 1) * P]
                    pe.matmul(to, hi, h[:, 0, j, :], start=(j == 0), stop=False)
                    pe.matmul(to, hi, h[:, 1, j, :], start=False, stop=False)
                    ins = pe.matmul(to, lo, h[:, 0, j, :], start=False, stop=(j == NT - 1))
                ins.then_inc(mm_done, 1)

            def unit(at, n, steps):
                wait(pe, u_free[n % 2], at.pairs + n // 2)
                for cols, left, right, start, stop in steps:
                    to = proj[:, n % 2, cols[0]:cols[1]]
                    if left is None:
                        ins = pe.transpose(to, right, ident[:, :])
                    else:
                        ins = pe.matmul(to, left, right, start=start, stop=stop)
                ins.then_inc(u_done, 1)

            def turned(blocks):
                return [((i * P, (i + 1) * P), None, b, True, True) for i, b in enumerate(blocks)]

            def summed(width, pairs, at=0):
                return [((at, at + width), l, r, i == 0, i == len(pairs) - 1) for i, (l, r) in enumerate(pairs)]

            def half_of(side, kind, j):
                if kind == "m":
                    return block_place(side, j)[3]
                return j // {"x": KF, "h": 4, "i": 4, "r": 1, "o": 2, "g": 4}[kind]

            def project(at, n, side, kind, j, half, fresh):
                tile = slice(j * P, (j + 1) * P)
                maker = {"Dm": ("x", KF * half + 1), "Dh": ("m", KH * half + 3), "Di": ("m", KH * half + 3),
                         "Fh": ("x", KF * half + 1), "Cm": ("g", 4 * half + 3), "Ch": ("m", KF * half + 1),
                         "Fr": ("h", 4 * j + 3), "Cr": ("h", 4 * j + 3), "Dr": ("h", 4 * j + 3)}.get(side + kind)
                if fresh and maker:
                    made = at.made(*maker, side)
                    wait(pe, u_free[1 - n % 2], at.pairs + (made + n % 2) // 2)
                if kind == "x":
                    c = j % 2
                    if fresh and side == "F":
                        pe.wait_ge(x_loaded, 16 * (at.batch + 2))
                    elif fresh:
                        own = at if PLAN[at.p][0] == "B" else at.prev
                        whole = at.p == "D" or half == 1
                        pe.wait_ge(ln_done, own.masked + (NT if whole else NT // 2))
                    src = x_nat if side == "F" else x1
                    unit(at, n, turned([src[:, 4 * half + i, c * P:(c + 1) * P] for i in range(4)]))
                elif kind == "m":
                    m = block_place(side, j)[2]
                    cols = slice(half * HALF, (half + 1) * HALF)
                    w, src, k = (w1s, xT, KF) if side == "D" else (w2s, rT, KH)
                    unit(at, n, summed(HALF, [(w[:, c, m * P:(m + 1) * P], src[:, c, cols]) for c in range(k)]))
                elif kind in "hi":
                    w, src, k = {"D": (wfce, rT, KH), "F": (w0e, xT, KF), "C": (whe, xT, KF)}[side]
                    cols = h_cols(side, kind, 3)
                    unit(at, n, summed(cols.stop - cols.start, [(src[:, c, tile], w[:, c, cols]) for c in range(k)]))
                elif kind == "r":
                    unit(at, n, turned([fcol[:, F_OF[side], 4 * j + i, 1:2].to_broadcast([P, P]) for i in range(4)]))
                elif kind == "o":
                    unit(at, n, turned([xT[:, c, t * P:(t + 1) * P] for t in (2 * j, 2 * j + 1) for c in range(KF)]))
                elif kind == "g":
                    own = at if PLAN[at.p][0] == "A" else at.prev
                    pe.wait_ge(elu_done, own.elu + j + 1)
                    unit(at, n, turned([pos_part[:, j % 2, m * P:(m + 1) * P] for m in range(KH)]))

            def phase(at, nxt):
                for s, att, work in steps_of(at):
                    if att:
                        if s == 0:
                            evacuated(pe, at.prev, at.prev.whole_h())
                        weigh(att, at, s)
                        there = at_distance(at, s + 2, nxt)
                        if there:
                            turn_prob(*there)
                    seen = set()
                    for n, side, kind, j in work:
                        half = half_of(side, kind, j)
                        project(at, n, side, kind, j, half, (side, kind, half) not in seen)
                        seen.add((side, kind, half))

            pe.wait_ge(s_id, 1)
            pe.wait_ge(s_wa, 1)
            def ahead(name, at):
                turn_prob(name, at, 0)
                turn_prob(name, at, 1)

            walk(pe, batches, phase, ahead)

        @block.vector
        def _(dve):
            dve.wait_ge(s_load, 16 * 10)
            flat_res = x1_res[:, :, :].rearrange("p t f -> p (t f)")
            n = 0
            for w, cols, a_at, fan, k in ((w0e, w0e[:, :, feat:], 0, feat, KF), (wfce, wfce[:, :, hid:], 2 * feat, hid, KH),
                                          (whe, whe[:, :, feat:], 2 * feat + 2 * hid, feat, KF)):
                for c in range(k):
                    for part in range(2):
                        wait(dve, s_wa_steps, n)
                        dve.tensor_tensor_reduce(neg_part[:, 0, 0:fan], w[:, c, 0:fan],
                                                 flat_res[:, a_at + part * fan:a_at + (part + 1) * fan], 1.0, 0.0,
                                                 ALU.mult, ALU.add, cols[:, c, part:part + 1]).then_inc(s_wa_steps, 1)
                        n += 1
            dve.wait_ge(s_wa_steps, n)
            for cols in (w0e[:, :, feat:], wfce[:, :, hid:], whe[:, :, feat:]):
                dve.tensor_scalar(cols[:, :, 2:3], cols[:, :, 0:1], SLOPE, None, ALU.mult).then_inc(s_wa_steps, 1)
            dve.wait_ge(s_wa_steps, n + 3)
            for half in range(2):
                dve.wait_ge(s_adj, 16 * (half + 1))
                dve.tensor_scalar(mask_add[:, 4 * half:4 * half + 4, :], rT[:, :, :].bitcast(I32), 0.0, MASKED,
                                  ALU.is_le, ALU.mult).then_inc(s_mask, 1)
            dve.wait_ge(s_mask, 2)
            dve.memset(minus_one[:, :], -1.0).then_inc(s_wa, 1)

            def score(name, at, t):
                layer, z = LAYER[name], zbuf[:, t % 2, :]
                dve.wait_ge(w_done, at.tile + t + 1)
                dve.scalar_tensor_tensor(out=z, in0=f2b[:, layer, :], scalar=fcol[:, layer, t, 0:1], in1=z, op0=ALU.add,
                                         op1=ALU.max).then_inc(z_done if name == "A" else leaky_done, 1)

            def masked_score(at, t):
                z = zbuf[:, t % 2, :]
                dve.tensor_tensor_reduce(z, z, mask_add[:, t, :], 1.0, LOWEST, ALU.add, ALU.max,
                                         row_max[:, t:t + 1]).then_inc(masked_done, 1)

            def minus_max(at, t):
                dve.wait_ge(masked_done, at.masked + t + 1)
                dve.tensor_scalar(neg_max[:, t:t + 1], row_max[:, t:t + 1], -1.0, None, ALU.mult).then_inc(z_done, 1)

            def turned_lo(name, at, t):
                dve.wait_ge(hi_done, at.tile + t + 1)
                dve.tensor_tensor(pT_lo[:, t % 2, :], p_turn[:, t % 2, :], pT_hi[:, t % 2, :].bitcast(F32),
                                  ALU.subtract).then_inc(lo_done, 1)

            def row_scale(at, t):
                dve.wait_ge(mm_done, at.tile + t + 1)
                dve.reciprocal(rden[:, t:t + 1], den[:, t:t + 1]).then_inc(rd_done, 1)

            def elu_parts(name, at, t):
                w = WIDTH[name]
                dve.wait_ge(rd_done, at.tile + t + 1)
                wait(dve, elu_done, at.elu + t - 1)
                dve.tensor_scalar(neg_part[:, t % 2, 0:w], acc[:, t % 2, 0:w], rden[:, t:t + 1], 0.0,
                                  ALU.mult, ALU.min).then_inc(neg_done, 1)
                if name == "A" and t >= 2:
                    dve.wait_ge(u_done, at.unit + at.index("g", t - 2) + 1)
                elif name == "E" and t < 2:
                    dve.wait_ge(u_done, at.unit)
                else:
                    wait(dve, sum_done, at.resid + t - 1)
                dve.tensor_scalar(pos_part[:, t % 2, 0:w], acc[:, t % 2, 0:w], rden[:, t:t + 1], 0.0,
                                  ALU.mult, ALU.max).then_inc(acc_free, 1)

            def elu_sum(name, at, t):
                w = WIDTH[name]
                dve.wait_ge(e2_done, at.elu + t + 1)
                if name == "E":
                    dve.wait_ge(res_done, at.resid + t + 1)
                else:
                    dve.wait_ge(acc_free, at.tile + t + 1)
                dve.scalar_tensor_tensor(out=pos_part[:, t % 2, 0:w], in0=neg_part[:, t % 2, 0:w], scalar=-1.0,
                                         in1=pos_part[:, t % 2, 0:w], op0=ALU.add, op1=ALU.add).then_inc(elu_done, 1)

            def add_r(at, n, t):
                dve.wait_ge(u_done, at.unit + n + 1)
                cols = rT[:, :, t * P:(t + 1) * P]
                dve.tensor_tensor(cols, proj[:, n % 2, :].rearrange("p (m i) -> p m i", m=KH), cols,
                                  ALU.add).then_inc(u_free[n % 2], 1)

            def normed(at, t, y):
                dve.wait_ge(rstd_done, at.masked + t + 1)
                dve.tensor_scalar(y, y, mv[:, t, 0:1], rstd[:, t:t + 1], ALU.subtract, ALU.mult).then_inc(ln_done, 1)

            def add_x(at, t):
                dve.wait_ge(rd_done, at.tile + t + 1)
                if t == 0:
                    wait(dve, x1_copied, 16 * (at.batch + 1))
                dve.scalar_tensor_tensor(out=x1[:, t, :], in0=acc[:, t % 2, 0:feat], scalar=rden[:, t:t + 1],
                                         in1=x_nat[:, t, :], op0=ALU.mult, op1=ALU.add).then_inc(acc_free, 1)

            def block_out(at, t):
                dve.wait_ge(elu_done, at.elu + t + 1)
                if t == 0:
                    dve.wait_ge(x1_copied, 16 * (at.batch + 1))
                dve.scalar_tensor_tensor(out=x1_res[:, t, :], in0=pos_part[:, t % 2, 0:feat], scalar=0.0,
                                         in1=x1_res[:, t, :], op0=ALU.max, op1=ALU.add).then_inc(sum_done, 1)

            def unit(at, n, dst, src=None):
                dve.wait_ge(u_done, at.unit + n + 1)
                dve.tensor_copy(dst, proj[:, n % 2, :] if src is None else src).then_inc(u_free[n % 2], 1)

            def f_whole(at, n, done):
                evacuated(dve, at, n)
                dve.tensor_copy(spare[:, 0:1], f2b[:, 0, 0:1]).then_inc(done, 1)

            def full_max(at, n):
                evacuated(dve, at, n)
                dve.tensor_reduce(f2_max[:, :], f2b[:, FC, :], AX.X, ALU.max).then_inc(fc_top_done, 1)
                dve.wait_ge(fc_top_done, 2 * at.f_full + 1)
                dve.tensor_scalar(neg_top_fc[:, :], fcol[:, FC, :, 0], f2_max[:, 0:1], -1.0,
                                  ALU.add, ALU.mult).then_inc(fc_top_done, 1)
                dve.wait_ge(fc_top_done, 2 * at.f_full + 2)
                dve.scalar_tensor_tensor(out=neg_max_fc[:, :], in0=neg_top_fc[:, :], scalar=SLOPE,
                                         in1=neg_top_fc[:, :], op0=ALU.mult, op1=ALU.min).then_inc(full_f_done, 1)

            def evacuate(at, n, side, kind, j):
                if kind in "hi":
                    h, cols = H_OF[side], h_cols(side, kind)
                    dve.wait_ge(u_hi, at.split + at.splits(n) + 1)
                    ins = dve.tensor_tensor(h[:, 1, j, cols], proj[:, n % 2, 0:feat], h[:, 0, j, cols].bitcast(F32),
                                            ALU.subtract)
                    if kind == "h":
                        ins = dve.tensor_copy(fcol[:, F_OF[side], j, :], proj[:, n % 2, feat:feat + 3])
                    ins.then_inc(u_free[n % 2], 1)
                elif kind == "g":
                    add_r(at, n, j)
                elif by_scalar(at, n):
                    pass
                elif kind == "x":
                    unit(at, n, xT[:, j % 2, (j // 2) * HALF:(j // 2 + 1) * HALF])
                elif kind == "m":
                    dst, bias, m, half = block_place(side, j)
                    dve.wait_ge(u_done, at.unit + n + 1)
                    dve.tensor_scalar(dst[:, m, half * HALF:(half + 1) * HALF], proj[:, n % 2, :], bias[:, m:m + 1], 0.0,
                                      ALU.add, ALU.max).then_inc(u_free[n % 2], 1)
                elif kind == "r":
                    unit(at, n, f2b[:, F_OF[side], j * HALF:(j + 1) * HALF])
                elif kind == "o":
                    unit(at, n, o_nat[:, 2 * j:2 * j + 2, :].rearrange("p t f -> p (t f)"))
                if (kind, j) == ("r", 1):
                    if side == "D":
                        full_max(at, n + 1)
                    else:
                        f_whole(at, n + 1, graph_f_done if side == "F" else hand_f_done)

            def step(at, s, att, nxt):
                lo, sc = (at_distance(at, s + d, nxt) if att else None for d in (2, 3))
                summed, exped, whole = (at_distance(at, s - d) for d in (1, 2, 3))
                if sc:
                    score(*sc)
                masked = sc[1:] if sc and sc[0] != "A" else None
                if summed:
                    row_scale(*summed[1:])
                if masked:
                    dve.wait_ge(leaky_done, masked[0].masked + masked[1] + 1)
                if not summed:
                    if masked:
                        dve.tensor_copy(spare[:, 0:1], minus_one[:, :])
                elif summed[0] == "B":
                    add_x(*summed[1:])
                else:
                    elu_parts(*summed)
                if masked:
                    masked_score(*masked)
                due = None
                if summed and summed[0] == "B":
                    own, t = due = summed[1:]
                    dve.wait_ge(acc_free, own.tile + t + 1)
                    dve.bn_stats(stats[:, t, :], x1[:, t, :]).then_inc(bst_done, 1)
                if exped and exped[0] != "B":
                    elu_sum(*exped)
                if masked:
                    minus_max(*masked)
                if exped and exped[0] == "E":
                    own, t = due = exped[1:]
                    block_out(own, t)
                    dve.wait_ge(sum_done, own.resid + t + 1)
                    dve.bn_stats(stats[:, t, :], x1_res[:, t, :]).then_inc(bst_done, 1)
                if due:
                    dve.wait_ge(bst_done, due[0].masked + due[1] + 1)
                if exped and exped[0] == "B":
                    normed(*exped[1:], x1[:, exped[2], :])
                elif whole and whole[0] == "E":
                    normed(*whole[1:], x1_res[:, whole[2], :])
                elif due:
                    dve.tensor_copy(spare[:, 0:1], minus_one[:, :])
                if due:
                    dve.bn_aggr(mv[:, due[1], :], stats[:, due[1], :]).then_inc(stat_done, 1)
                if lo:
                    turned_lo(*lo)

            def phase(at, nxt):
                for s, att, work in steps_of(at):
                    step(at, s, att, nxt)
                    for unit_of in work:
                        evacuate(at, *unit_of)

            def ahead(name, at):
                for t in range(3):
                    if t == 2:
                        turned_lo(name, at, 0)
                        turned_lo(name, at, 1)
                    score(name, at, t)
                    if name != "A":
                        dve.wait_ge(leaky_done, at.masked + t + 1)
                        dve.tensor_copy(spare[:, 0:1], minus_one[:, :])
                        masked_score(at, t)
                        minus_max(at, t)

            walk(dve, batches, phase, ahead)


def kernel(**inputs):
    import numpy as np
    import concourse.bacc as bacc
    from concourse.bass_utils import run_bass_kernel_spmd

    order = ["x", "adj", "L0_gnn_W", "L0_gnn_a", "L1_gnn_mlp1_w", "L1_gnn_mlp1_b", "L1_gnn_mlp2_w", "L1_gnn_mlp2_b",
             "L1_gnn_W_fc", "L1_gnn_a_fc", "L1_gnn_W_hand", "L1_gnn_a_hand"]
    nc = bacc.Bacc("TRN2", target_bir_lowering=False, num_devices=1)
    arrays, args = {}, []
    for name in order:
        a = np.ascontiguousarray(inputs[name])
        arrays[f"in_{name}"] = a
        args.append(nc.dram_tensor(f"in_{name}", a.shape, mybir.dt.from_np(a.dtype), kind="ExternalInput").ap())
    out = nc.dram_tensor("out_x", arrays["in_x"].shape, F32, kind="ExternalOutput").ap()
    build(nc, *args, out)
    return run_bass_kernel_spmd(nc, [arrays], core_ids=[0]).results[0]["out_x"]
```

```python
from contextlib import ExitStack

import concourse.bass as bass
import concourse.mybir as mybir

F32 = mybir.dt.float32
F32R = mybir.dt.float32r
BF16 = mybir.dt.bfloat16
I32 = mybir.dt.int32
ACT = mybir.ActivationFunctionType
ALU = mybir.AluOpType
AX = mybir.AxisListType

P = 128
SLOPE = 0.2
MASKED = -9e15
EPS = 1e-5
LOWEST = -3.0e38

TILES = 8


def units(side, text):
    steps = []
    for step in text.split("|"):
        early, _, late = step.rpartition(">")
        early, late = ([(w[0], w[1], int(w[2:])) for w in (v if v[0].isupper() else side + v for v in part.split())]
                       for part in (early, late))
        steps.append((early + late, len(early)))
    return steps


PLAN = {
    "F": (None, units("F", "x0 x1 x2 x3|h0 h1 h2 h3 h4 h5 h6 h7|r0 r1")),
    "B": ("B", units("D", "||||||x0 x1 > m0 m1|m2 m3")),
    "D": (None, units("D", "|x2 x3 m4 m5 m6 m7|h0 h1 h2 h3 h4 h5 h6 h7|r0 r1|i0 i1 i2 i3 i4 i5 i6 i7")),
    "AF": ("A", units("F", "|x0 x1 > x2 x3|h0 h1 > h2 g0|h3 h4 > h5 g1|h6 h7 > r0 g2 r1|g3|g4|g5")),
    "BC": ("B", units("C", "m0 g6|m1 g7|h0 h1 > h2 m2|h3 > m3|h4 h5 h6 h7 > r0 r1|o0 o1 > o2 o3|"
                           "Dx0 Dx1 > Dm0 Dm1|Dm2 Dm3")),
    "ED": ("E", units("D", "h0 h1 > h2|h3 > i0|x2 x3 > i1 m4 m5|m6 > m7 i2 h4|h5 h6 > h7 r0 i3 r1|i4 > i5|i6 > i7|")),
    "A": ("A", units("F", "||g0|g1|g2|g3|g4|g5")),
    "C": (None, units("C", "m0 m1 g6|g7|h0 h1 h2 h3 m2 m3|h4 h5 h6 h7 r0 o0 o1 r1|o2 o3")),
    "E": ("E", units("E", "|||||||")),
    "end": (None, units("E", "||")),
}
ORDER = {p: [u for step, _ in steps for u in step] for p, (_, steps) in PLAN.items()}
FIRST = ["F", "ahead B", "B", "D", "ahead A"]
BODY = ["AF", "BC", "ED"]
LAST = ["A", "C", "ahead E", "E", "end"]
NEXT = {"AF": "B", "BC": "E", "ED": "A"}


def adds(p):
    att, n = PLAN[p][0], len(ORDER[p])
    assert n % 2 == 0
    return dict(tile=TILES * (att is not None), masked=TILES * (att in ("B", "E")), elu=TILES * (att in ("A", "E")),
                resid=TILES * (att == "E"), unit=n, pairs=n // 2, split=sum(k in "hi" for _, k, _ in ORDER[p]),
                f_graph=ORDER[p].count(("F", "r", 1)), f_hand=ORDER[p].count(("C", "r", 1)),
                f_full=ORDER[p].count(("D", "r", 1)))


NAMES = list(adds("F"))


def add(counts, phases):
    return {n: counts[n] + sum(adds(p)[n] for p in phases) for n in NAMES}


class At:

    def __init__(self, p, counts, batch, prev=None):
        self.p, self.counts, self.batch, self.prev = p, counts, batch, prev

    def __getattr__(self, name):
        return self.counts[name]

    def after(self):
        return At(None, add(self.counts, [self.p]), self.batch, self)

    def index(self, kind, n):
        return next(i for i, u in enumerate(ORDER[self.p]) if u[1:] == (kind, n))

    def made(self, kind, n, side):
        return next((i + 1 for i, u in enumerate(ORDER[self.p]) if u == (side, kind, n)), 0)

    def splits(self, n):
        return sum(u[1] in "hi" for u in ORDER[self.p][:n])

    def whole_h(self):
        return max(i + 1 for i, u in enumerate(ORDER[self.p]) if u[1] in "hi")


def walk(eng, batches, phase, ahead):

    def run(counts, k, items, prev):
        done = []
        for item in items:
            at = At(item, add(counts, done), k, prev)
            if item.startswith("ahead"):
                ahead(item[-1], at)
            else:
                phase(at, NEXT.get(item))
                done.append(item)
                prev = at

    zero = {n: 0 for n in NAMES}
    start = add(zero, ["F", "B", "D"])
    per = add(zero, BODY)

    def begin(k):
        return {n: k * per[n] + start[n] for n in NAMES}

    def begin_last(k):
        return {n: k * per[n] + (start[n] - adds("ED")[n]) for n in NAMES}

    run(zero, -1, FIRST, None)
    run(start, 0, BODY, At("D", add(zero, ["F", "B"]), -1))
    with eng.Fori(1, batches - 1) as k:
        run(begin(k), k, BODY, At("ED", begin_last(k), k - 1))
    k = batches - 1
    run(begin(k), k, LAST, At("ED", begin_last(k), k - 1))


def steps_of(at):
    att, steps = PLAN[at.p]
    n = 0
    for s, (step, early) in enumerate(steps):
        work = [(n + i, *u) for i, u in enumerate(step)]
        yield s, att, work[:early], work[early:]
        n += len(step)


def at_distance(at, s, nxt=None):
    att = PLAN[at.p][0]
    if 0 <= s < TILES and att:
        return att, at, s
    if s < 0 and at.prev and PLAN[at.prev.p][0]:
        return PLAN[at.prev.p][0], at.prev, s + TILES
    if s >= TILES and nxt:
        return nxt, at.after(), s - TILES
    return None


def wait(eng, sem, value):
    if isinstance(value, int) and value <= 0:
        return
    eng.wait_ge(sem, value)


def build(nc, x, adj, w0, a0, w1, b1, w2, b2, wfc, afc, wh, ah, out):
    batches, tokens, feat = x.shape
    hid = w1.shape[1]
    NT = tokens // P
    KF = feat // P
    KH = hid // P
    HALF = tokens // 2
    assert (NT, KF, KH, HALF) == (8, 2, 4, 512)
    G0, FC, HAND = 0, 1, 2
    LAYER = {"A": FC, "B": G0, "E": HAND}
    F_OF = {"D": FC, "F": G0, "C": HAND}
    WIDTH = {"A": hid, "B": feat, "E": feat}

    ctx = ExitStack()
    with ctx:
        def sb(name, shape, dt=F32):
            return ctx.enter_context(nc.sbuf_tensor(name, shape, dt))

        def pb(name, shape):
            return ctx.enter_context(nc.psum_tensor(name, shape, F32))

        def sem(name):
            return ctx.enter_context(nc.semaphore(name))

        w0e = sb("w0e", [P, KF, feat + 3])
        w1s = sb("w1s", [P, KF, hid])
        wfce = sb("wfce", [P, KH, hid + 3])
        w2s = sb("w2s", [P, KH, feat])
        whe = sb("whe", [P, KF, feat + 3])
        b1c = sb("b1c", [P, KH])
        b2c = sb("b2c", [P, KF])
        ident = sb("ident", [P, P])
        minus_half = sb("minus_half", [P, 1])
        eps = sb("eps", [P, 1])
        minus_one = sb("minus_one", [P, 1])
        mask_add = sb("mask_add", [P, NT, tokens], BF16)
        x_nat = sb("x_nat", [P, NT, feat])
        x1 = sb("x1", [P, NT, feat])
        x1_res = sb("x1_res", [P, NT, feat])
        o_nat = sb("o_nat", [P, NT, feat])
        h_wide = sb("h_wide", [P, 2, NT, hid], F32R)
        h_graph = sb("h_graph", [P, 2, NT, feat], F32R)
        h_hand = sb("h_hand", [P, 2, NT, feat], F32R)
        H = {"A": h_wide, "B": h_graph, "E": h_hand}
        H_OF = {"D": h_wide, "F": h_graph, "C": h_hand}
        xT = sb("xT", [P, KF, tokens])
        rT = sb("rT", [P, KH, tokens])
        fcol = sb("fcol", [P, 3, NT, 3])
        f2b = sb("f2b", [P, 3, tokens])
        zbuf = sb("zbuf", [P, 2, tokens])
        pT_hi = sb("pT_hi", [P, 2, tokens], F32R)
        pT_lo = sb("pT_lo", [P, 2, tokens], F32R)
        row_max = sb("row_max", [P, NT])
        neg_max = sb("neg_max", [P, NT])
        neg_max_fc = sb("neg_max_fc", [P, NT])
        neg_top_fc = sb("neg_top_fc", [P, NT])
        f2_max = sb("f2_max", [P, 1])
        den = sb("den", [P, NT])
        rden = sb("rden", [P, NT])
        neg_part = sb("neg_part", [P, 2, hid])
        pos_part = sb("pos_part", [P, 2, hid])
        stats = sb("stats", [P, NT, 6])
        spare = sb("spare", [P, NT])
        mv = sb("mv", [P, NT, 2])
        var_eps = sb("var_eps", [P, NT])
        rstd = sb("rstd", [P, NT])

        p_turn = pb("p_turn", [P, 2, tokens])
        acc = pb("acc", [P, 2, 512])
        proj = pb("proj", [P, 2, 512])

        s_load0 = sem("first_weights_loaded")
        s_load = sem("weights_loaded")
        s_adj = [sem(f"adj_loaded{i}") for i in range(3)]
        s_mask = sem("mask_built")
        s_wa0 = sem("first_weights_ready")
        s_wa = sem("weights_ready")
        s_wa_steps = sem("wa_steps")
        s_id0 = sem("ident_zeroed")
        s_id = sem("ident_ready")
        x_loaded = sem("x_loaded")
        x1_copied = sem("x1_copied")
        out_stored = sem("out_stored")
        masked_done = sem("masked_scores_done")
        w_done = sem("sloped_scores_done")
        leaky_done = sem("leaky_scores_done")
        fc_top_done = sem("fc_top_done")
        full_f_done = sem("full_f_done")
        z_done = sem("scores_done")
        graph_f_done = sem("graph_f_done")
        hand_f_done = sem("hand_f_done")
        p_done = sem("prob_done")
        t_done = sem("prob_turned")
        hi_done = sem("prob_hi_done")
        lo_done = sem("prob_lo_done")
        mm_done = sem("attention_summed")
        rd_done = sem("rden_done")
        acc_free = sem("acc_read")
        neg_done = sem("neg_part_done")
        e1_done = sem("first_exp_done")
        e2_done = sem("second_exp_done")
        elu_done = sem("elu_done")
        res_done = sem("residual_added")
        sum_done = sem("block_sum_done")
        bst_done = sem("bn_stats_done")
        stat_done = sem("mean_var_done")
        veps_done = sem("var_eps_done")
        rstd_done = sem("rstd_done")
        ln_done = sem("layer_norm_done")
        u_done = sem("unit_summed")
        u_hi = sem("unit_hi_done")
        u_free = [sem("bank0_read"), sem("bank1_read")]

        adj_stage = [(rT[:, :, :].bitcast(I32), slice(0, 4))]
        for half, buf in enumerate((x1, o_nat)):
            adj_stage.append((buf[:, :, :].bitcast(I32).rearrange("p (t a) f -> p t (a f)", t=2),
                              slice(4 + 2 * half, 6 + 2 * half)))

        def block_place(side, j):
            return (rT, b1c, j % KH, j // KH) if side == "D" else (xT, b2c, j % KF, j // KF)

        def h_cols(side, kind, more=0):
            if side == "D":
                return slice(0, feat) if kind == "i" else slice(feat, hid + more)
            return slice(0, feat + more)

        def by_scalar(at, n):
            return n % 2 == 0 or at.p in ("F", "B", "D", "BC", "ED")

        def evacuated(eng, at, n):
            wait(eng, u_free[0], at.pairs + (n + 1) // 2)
            wait(eng, u_free[1], at.pairs + n // 2)

        block = ctx.enter_context(nc.Block())

        @block.sync
        def _(sp):
            vectors = [(a0, 0), (afc, 2 * feat), (ah, 2 * feat + 2 * hid)]
            flat_res = x1_res[:, :, :].rearrange("p t f -> p (t f)")
            sp.dma_start(x_nat[:, :, :], x[0].rearrange("(t p) f -> p t f", p=P)).then_inc(x_loaded, 16)
            sp.dma_start(w0e[:, :, 0:feat], w0.rearrange("(k p) n -> p k n", p=P)).then_inc(s_load0, 16)
            for a, at in vectors:
                n = a.shape[0]
                sp.dma_start(flat_res[:, at:at + n], a.rearrange("n o -> (o n)").partition_broadcast(P)).then_inc(
                    s_load0 if at == 0 else s_load, 16)
            adj_t = adj.rearrange("(t p) j -> p t j", p=P)
            for (stage, tiles), loaded in zip(adj_stage, s_adj):
                sp.dma_start(stage, adj_t[:, tiles, :]).then_inc(loaded, 16)
            sp.dma_start(w1s[:, :, :], w1.rearrange("(k p) n -> p k n", p=P)).then_inc(s_load, 16)
            sp.dma_start(wfce[:, :, 0:hid], wfc.rearrange("(k p) n -> p k n", p=P)).then_inc(s_load, 16)
            sp.dma_start(whe[:, :, 0:feat], wh.rearrange("(k p) n -> p k n", p=P)).then_inc(s_load, 16)
            sp.dma_start(w2s[:, :, :], w2.rearrange("(k p) n -> p k n", p=P)).then_inc(s_load, 16)
            with nc.allow_non_contiguous_dma(reason="768 bias values, once"):
                sp.dma_start(b1c[:, :], b1.rearrange("(k p) -> p k", p=P)).then_inc(s_load, 16)
                sp.dma_start(b2c[:, :], b2.rearrange("(k p) -> p k", p=P)).then_inc(s_load, 16)

            def store(b, masked):
                sp.wait_ge(ln_done, masked)
                sp.dma_start(out[b].rearrange("(t p) f -> p t f", p=P) if isinstance(b, int) else
                             out[bass.ds(b, 1)].rearrange("o (t p) f -> p (o t) f", p=P),
                             x1_res[:, :, :]).then_inc(out_stored, 16)

            def phase(at, nxt):
                b = at.batch
                if at.p == "AF":
                    sp.wait_ge(acc_free, at.tile if isinstance(b, int) and b == 0 else at.tile - TILES)
                    sp.dma_start(x_nat[:, :, :], x[b + 1].rearrange("(t p) f -> p t f", p=P) if isinstance(b, int) else
                                 x[bass.ds(b + 1, 1)].rearrange("o (t p) f -> p (o t) f", p=P)).then_inc(x_loaded, 16)
                if at.p in ("AF", "A"):
                    if isinstance(b, int) and b == 0:
                        sp.wait_ge(ln_done, at.masked)
                        sp.wait_ge(s_wa, 1)
                    else:
                        store(b - 1, at.masked)
                        sp.wait_ge(out_stored, 16 * b)
                    sp.dma_start(x1_res[:, :, :], x1[:, :, :]).then_inc(x1_copied, 16)
                if at.p == "end":
                    store(b, at.masked)

            walk(sp, batches, phase, lambda name, at: None)
            sp.wait_ge(out_stored, 16 * batches)

        @block.gpsimd
        def _(pool):
            pool.memset(minus_half[:, :], -0.5)
            pool.memset(eps[:, :], EPS)
            pool.memset(minus_one[:, :], -1.0).then_inc(s_id0, 1)
            pool.memset(ident[:, :], 0.0).then_inc(s_id0, 1)
            pool.wait_ge(s_id0, 2)
            pool.affine_select(out=ident[:, :], in_=ident[:, :], compare_op=ALU.not_equal, fill=1.0, base=0,
                               pattern=[[-1, P]], channel_multiplier=1).then_inc(s_id, 1)
            pool.wait_ge(s_id, 1)

            def residual(at, t):
                pool.wait_ge(acc_free, at.tile + t + 1)
                g = pos_part[:, t % 2, 0:feat]
                pool.tensor_tensor(g, g, o_nat[:, t, :], ALU.add).then_inc(res_done, 1)

            def inverse_deviation(at, t):
                pool.wait_ge(stat_done, at.masked + t + 1)
                pool.tensor_tensor(var_eps[:, t:t + 1], mv[:, t, 1:2], eps[:, :], ALU.add).then_inc(veps_done, 1)
                pool.wait_ge(veps_done, at.masked + t + 1)
                pool.tensor_tensor(rstd[:, t:t + 1], var_eps[:, t:t + 1], minus_half[:, :], ALU.pow).then_inc(rstd_done, 1)

            def phase(at, nxt):
                if PLAN[at.p][0] == "B":
                    for t in range(NT):
                        inverse_deviation(at, t)
                elif PLAN[at.p][0] == "E":
                    for t in range(NT + 1):
                        if t < NT:
                            residual(at, t)
                        if t > 0:
                            inverse_deviation(at, t - 1)

            walk(pool, batches, phase, lambda name, at: None)

        @block.scalar
        def _(act):
            def sloped_tile(name, at, t):
                layer = LAYER[name]
                if t == 0:
                    f_ready(name, at)
                wait(act, t_done, at.tile + t - 1)
                act.activation(zbuf[:, t % 2, :], f2b[:, layer, :], ACT.Identity, bias=fcol[:, layer, t, 2:3],
                               scale=SLOPE).then_inc(w_done, 1)

            def f_ready(name, at):
                done, n = {"A": (full_f_done, at.f_full), "B": (graph_f_done, at.f_graph),
                           "E": (hand_f_done, at.f_hand)}[name]
                act.wait_ge(done, n)

            def prob_tile(name, at, t):
                slot, top = t % 2, neg_max_fc if name == "A" else neg_max
                act.wait_ge(z_done, at.tile + t + 1)
                act.activation(zbuf[:, slot, :], zbuf[:, slot, :], ACT.Exp, bias=top[:, t:t + 1],
                               accum_out=den[:, t:t + 1]).then_inc(p_done, 1)

            def turned_hi(name, at, t):
                act.wait_ge(t_done, at.tile + t + 1)
                wait(act, mm_done, at.tile + t - 1)
                act.activation(pT_hi[:, t % 2, :], p_turn[:, t % 2, :], ACT.Copy).then_inc(hi_done, 1)

            def elu_exps(name, at, t):
                part = neg_part[:, t % 2, 0:WIDTH[name]]
                act.wait_ge(neg_done, at.elu + t + 1)
                act.activation(part, part, ACT.Exp).then_inc(e1_done, 1)
                act.wait_ge(e1_done, at.elu + t + 1)
                act.activation(part, part, ACT.Exp, bias=minus_one[:, :]).then_inc(e2_done, 1)

            def unit(at, n, dst, func=ACT.Copy, width=512, last=True, **more):
                act.wait_ge(u_done, at.unit + n + 1)
                ins = act.activation(dst, proj[:, n % 2, 0:width], func, **more)
                ins.then_inc(u_free[n % 2] if last else u_hi, 1)

            def evacuate(at, n, side, kind, j):
                if kind in "hi":
                    h, cols = H_OF[side], h_cols(side, kind)
                    unit(at, n, h[:, 0, j, cols], width=feat, last=False)
                elif kind == "g" or not by_scalar(at, n):
                    return
                elif kind == "x":
                    unit(at, n, xT[:, j % 2, (j // 2) * HALF:(j // 2 + 1) * HALF])
                elif kind == "m":
                    dst, bias, m, half = block_place(side, j)
                    unit(at, n, dst[:, m, half * HALF:(half + 1) * HALF], ACT.Relu, bias=bias[:, m:m + 1])
                elif kind == "r":
                    unit(at, n, f2b[:, F_OF[side], j * HALF:(j + 1) * HALF])
                elif kind == "o":
                    unit(at, n, o_nat[:, 2 * j:2 * j + 2, :].rearrange("p t f -> p (t f)"))

            def phase(at, nxt):
                for s, att, early, late in steps_of(at):
                    ready, turned, later = (at_distance(at, s + d, nxt) if att else None for d in (2, 2, 4))
                    if ready:
                        prob_tile(*ready)
                    there = at_distance(at, s - 1)
                    if there and there[0] != "B":
                        elu_exps(*there)
                    if nxt and s == NT - 3:
                        sloped_tile(*at_distance(at, NT, nxt))
                    for unit_of in early:
                        evacuate(at, *unit_of)
                    if turned:
                        turned_hi(*turned)
                    if later and later[2] > 0:
                        sloped_tile(*later)
                    for unit_of in late:
                        evacuate(at, *unit_of)

            act.wait_ge(s_id, 1)

            def ahead(name, at):
                if name == "B":
                    act.wait_ge(s_load, 16 * 8)
                sloped_tile(name, at, 0)
                sloped_tile(name, at, 1)
                for t in range(2):
                    prob_tile(name, at, t)
                for t in range(2):
                    turned_hi(name, at, t)
                sloped_tile(name, at, 2)
                sloped_tile(name, at, 3)

            walk(act, batches, phase, ahead)

        @block.tensor
        def _(pe):
            def turn_prob(name, at, t):
                slot = t % 2
                pe.wait_ge(p_done, at.tile + t + 1)
                wait(pe, lo_done, at.tile + t - 1)
                for j in range(NT):
                    ins = pe.transpose(p_turn[:, slot, j * P:(j + 1) * P], zbuf[:, slot, j * P:(j + 1) * P], ident[:, :])
                ins.then_inc(t_done, 1)

            def weigh(name, at, t):
                slot, h, w = t % 2, H[name], WIDTH[name]
                pe.wait_ge(lo_done, at.tile + t + 1)
                wait(pe, acc_free, at.tile + t - 1)
                to = acc[:, slot, 0:w]
                for j in range(NT):
                    hi, lo = pT_hi[:, slot, j * P:(j + 1) * P], pT_lo[:, slot, j * P:(j + 1) * P]
                    pe.matmul(to, hi, h[:, 0, j, :], start=(j == 0), stop=False)
                    pe.matmul(to, hi, h[:, 1, j, :], start=False, stop=False)
                    ins = pe.matmul(to, lo, h[:, 0, j, :], start=False, stop=(j == NT - 1))
                ins.then_inc(mm_done, 1)

            def unit(at, n, steps):
                wait(pe, u_free[n % 2], at.pairs + n // 2)
                for cols, left, right, start, stop in steps:
                    to = proj[:, n % 2, cols[0]:cols[1]]
                    if left is None:
                        ins = pe.transpose(to, right, ident[:, :])
                    else:
                        ins = pe.matmul(to, left, right, start=start, stop=stop)
                ins.then_inc(u_done, 1)

            def turned(blocks):
                return [((i * P, (i + 1) * P), None, b, True, True) for i, b in enumerate(blocks)]

            def summed(width, pairs, at=0):
                return [((at, at + width), l, r, i == 0, i == len(pairs) - 1) for i, (l, r) in enumerate(pairs)]

            def half_of(side, kind, j):
                if kind == "m":
                    return block_place(side, j)[3]
                return j // {"x": KF, "h": 4, "i": 4, "r": 1, "o": 2, "g": 4}[kind]

            def project(at, n, side, kind, j, half, fresh):
                tile = slice(j * P, (j + 1) * P)
                maker = {"Dm": ("x", KF * half + 1), "Dh": ("m", KH * half + 3), "Di": ("m", KH * half + 3),
                         "Fh": ("x", KF * half + 1), "Cm": ("g", 4 * half + 3), "Ch": ("m", KF * half + 1),
                         "Fr": ("h", 4 * j + 3), "Cr": ("h", 4 * j + 3), "Dr": ("h", 4 * j + 3)}.get(side + kind)
                if fresh and maker:
                    made = at.made(*maker, side)
                    wait(pe, u_free[1 - n % 2], at.pairs + (made + n % 2) // 2)
                if kind == "x":
                    c = j % 2
                    if fresh and side == "F":
                        pe.wait_ge(x_loaded, 16 * (at.batch + 2))
                    elif fresh:
                        own = at if PLAN[at.p][0] == "B" else at.prev
                        pe.wait_ge(ln_done, own.masked + (half + 1) * NT // 2)
                    src = x_nat if side == "F" else x1
                    unit(at, n, turned([src[:, 4 * half + i, c * P:(c + 1) * P] for i in range(4)]))
                elif kind == "m":
                    m = block_place(side, j)[2]
                    cols = slice(half * HALF, (half + 1) * HALF)
                    w, src, k = (w1s, xT, KF) if side == "D" else (w2s, rT, KH)
                    unit(at, n, summed(HALF, [(w[:, c, m * P:(m + 1) * P], src[:, c, cols]) for c in range(k)]))
                elif kind in "hi":
                    if at.p in ("F", "D") and kind == "h" and fresh:
                        pe.wait_ge(s_wa0 if at.p == "F" else s_wa, 1)
                    w, src, k = {"D": (wfce, rT, KH), "F": (w0e, xT, KF), "C": (whe, xT, KF)}[side]
                    cols = h_cols(side, kind, 3)
                    unit(at, n, summed(cols.stop - cols.start, [(src[:, c, tile], w[:, c, cols]) for c in range(k)]))
                elif kind == "r":
                    unit(at, n, turned([fcol[:, F_OF[side], 4 * j + i, 1:2].to_broadcast([P, P]) for i in range(4)]))
                elif kind == "o":
                    unit(at, n, turned([xT[:, c, t * P:(t + 1) * P] for t in (2 * j, 2 * j + 1) for c in range(KF)]))
                elif kind == "g":
                    own = at if PLAN[at.p][0] == "A" else at.prev
                    pe.wait_ge(elu_done, own.elu + j + 1)
                    unit(at, n, turned([pos_part[:, j % 2, m * P:(m + 1) * P] for m in range(KH)]))

            def phase(at, nxt):
                for s, att, early, late in steps_of(at):
                    if att:
                        if s == 0:
                            evacuated(pe, at.prev, at.prev.whole_h())
                        weigh(att, at, s)
                    seen = set()
                    for work in (early, late):
                        for n, side, kind, j in work:
                            half = half_of(side, kind, j)
                            project(at, n, side, kind, j, half, (side, kind, half) not in seen)
                            seen.add((side, kind, half))
                        there = at_distance(at, s + 2, nxt) if att and work is early else None
                        if there:
                            turn_prob(*there)

            pe.wait_ge(s_id, 1)

            def ahead(name, at):
                if name == "B":
                    pe.wait_ge(s_load, 16 * 8)
                turn_prob(name, at, 0)
                turn_prob(name, at, 1)

            walk(pe, batches, phase, ahead)

        @block.vector
        def _(dve):
            def times_a(w, cols, a_at, fan, k, n):
                flat_res = x1_res[:, :, :].rearrange("p t f -> p (t f)")
                for c in range(k):
                    for part in range(2):
                        wait(dve, s_wa_steps, n)
                        dve.tensor_tensor_reduce(neg_part[:, 0, 0:fan], w[:, c, 0:fan],
                                                 flat_res[:, a_at + part * fan:a_at + (part + 1) * fan], 1.0, 0.0,
                                                 ALU.mult, ALU.add, cols[:, c, part:part + 1]).then_inc(s_wa_steps, 1)
                        n += 1
                dve.wait_ge(s_wa_steps, n)
                return n

            def sloped_column(cols):
                return dve.tensor_scalar(cols[:, :, 2:3], cols[:, :, 0:1], SLOPE, None, ALU.mult)

            dve.wait_ge(s_load0, 16 * 2)
            first_steps = times_a(w0e, w0e[:, :, feat:], 0, feat, KF, 0)
            sloped_column(w0e[:, :, feat:]).then_inc(s_wa0, 1)

            def make_mask():
                for (stage, tiles), loaded in zip(adj_stage, s_adj):
                    dve.wait_ge(loaded, 16)
                    dve.tensor_scalar(mask_add[:, tiles, :], stage, 0.0, MASKED, ALU.is_le, ALU.mult).then_inc(s_mask, 1)
                dve.wait_ge(s_mask, len(adj_stage))

            def other_score_columns():
                dve.wait_ge(s_load, 16 * 8)
                n = times_a(wfce, wfce[:, :, hid:], 2 * feat, hid, KH, first_steps)
                times_a(whe, whe[:, :, feat:], 2 * feat + 2 * hid, feat, KF, n)
                for cols in (wfce[:, :, hid:], whe[:, :, feat:]):
                    last = sloped_column(cols)
                last.then_inc(s_wa, 1)

            def score(name, at, t):
                layer, z = LAYER[name], zbuf[:, t % 2, :]
                dve.wait_ge(w_done, at.tile + t + 1)
                dve.scalar_tensor_tensor(out=z, in0=f2b[:, layer, :], scalar=fcol[:, layer, t, 0:1], in1=z, op0=ALU.add,
                                         op1=ALU.max).then_inc(z_done if name == "A" else leaky_done, 1)

            def masked_score(at, t):
                z = zbuf[:, t % 2, :]
                dve.tensor_tensor_reduce(z, z, mask_add[:, t, :], 1.0, LOWEST, ALU.add, ALU.max,
                                         row_max[:, t:t + 1]).then_inc(masked_done, 1)

            def minus_max(at, t):
                dve.wait_ge(masked_done, at.masked + t + 1)
                dve.tensor_scalar(neg_max[:, t:t + 1], row_max[:, t:t + 1], -1.0, None, ALU.mult).then_inc(z_done, 1)

            def whole_score(name, at, t):
                score(name, at, t)
                if name != "A":
                    dve.wait_ge(leaky_done, at.masked + t + 1)
                    dve.tensor_copy(spare[:, 0:1], minus_one[:, :])
                    masked_score(at, t)
                    minus_max(at, t)

            def turned_lo(name, at, t):
                dve.wait_ge(hi_done, at.tile + t + 1)
                dve.tensor_tensor(pT_lo[:, t % 2, :], p_turn[:, t % 2, :], pT_hi[:, t % 2, :].bitcast(F32),
                                  ALU.subtract).then_inc(lo_done, 1)

            def row_scale(at, t):
                dve.wait_ge(mm_done, at.tile + t + 1)
                dve.reciprocal(rden[:, t:t + 1], den[:, t:t + 1]).then_inc(rd_done, 1)

            def elu_parts(name, at, t):
                w = WIDTH[name]
                dve.wait_ge(rd_done, at.tile + t + 1)
                wait(dve, elu_done, at.elu + t - 1)
                dve.tensor_scalar(neg_part[:, t % 2, 0:w], acc[:, t % 2, 0:w], rden[:, t:t + 1], 0.0,
                                  ALU.mult, ALU.min).then_inc(neg_done, 1)
                if name == "A" and t >= 2:
                    dve.wait_ge(u_done, at.unit + at.index("g", t - 2) + 1)
                elif name == "E" and t < 2:
                    dve.wait_ge(u_done, at.unit)
                else:
                    wait(dve, sum_done, at.resid + t - 1)
                dve.tensor_scalar(pos_part[:, t % 2, 0:w], acc[:, t % 2, 0:w], rden[:, t:t + 1], 0.0,
                                  ALU.mult, ALU.max).then_inc(acc_free, 1)

            def elu_sum(name, at, t):
                w = WIDTH[name]
                dve.wait_ge(e2_done, at.elu + t + 1)
                if name == "E":
                    dve.wait_ge(res_done, at.resid + t + 1)
                else:
                    dve.wait_ge(acc_free, at.tile + t + 1)
                dve.scalar_tensor_tensor(out=pos_part[:, t % 2, 0:w], in0=neg_part[:, t % 2, 0:w], scalar=-1.0,
                                         in1=pos_part[:, t % 2, 0:w], op0=ALU.add, op1=ALU.add).then_inc(elu_done, 1)

            def add_r(at, n, t):
                dve.wait_ge(u_done, at.unit + n + 1)
                cols = rT[:, :, t * P:(t + 1) * P]
                dve.tensor_tensor(cols, proj[:, n % 2, :].rearrange("p (m i) -> p m i", m=KH), cols,
                                  ALU.add).then_inc(u_free[n % 2], 1)

            def normed(at, t, y):
                dve.wait_ge(rstd_done, at.masked + t + 1)
                dve.tensor_scalar(y, y, mv[:, t, 0:1], rstd[:, t:t + 1], ALU.subtract, ALU.mult).then_inc(ln_done, 1)

            def add_x(at, t):
                dve.wait_ge(rd_done, at.tile + t + 1)
                if t == 0:
                    wait(dve, x1_copied, 16 * (at.batch + 1))
                dve.scalar_tensor_tensor(out=x1[:, t, :], in0=acc[:, t % 2, 0:feat], scalar=rden[:, t:t + 1],
                                         in1=x_nat[:, t, :], op0=ALU.mult, op1=ALU.add).then_inc(acc_free, 1)

            def block_out(at, t):
                dve.wait_ge(elu_done, at.elu + t + 1)
                if t == 0:
                    dve.wait_ge(x1_copied, 16 * (at.batch + 1))
                dve.scalar_tensor_tensor(out=x1_res[:, t, :], in0=pos_part[:, t % 2, 0:feat], scalar=0.0,
                                         in1=x1_res[:, t, :], op0=ALU.max, op1=ALU.add).then_inc(sum_done, 1)

            def unit(at, n, dst, src=None):
                dve.wait_ge(u_done, at.unit + n + 1)
                dve.tensor_copy(dst, proj[:, n % 2, :] if src is None else src).then_inc(u_free[n % 2], 1)

            def f_whole(at, n, done):
                evacuated(dve, at, n)
                dve.tensor_copy(spare[:, 0:1], f2b[:, 0, 0:1]).then_inc(done, 1)

            def full_max(at, n):
                evacuated(dve, at, n)
                dve.tensor_reduce(f2_max[:, :], f2b[:, FC, :], AX.X, ALU.max).then_inc(fc_top_done, 1)
                dve.wait_ge(fc_top_done, 2 * at.f_full + 1)
                dve.tensor_scalar(neg_top_fc[:, :], fcol[:, FC, :, 0], f2_max[:, 0:1], -1.0,
                                  ALU.add, ALU.mult).then_inc(fc_top_done, 1)
                dve.wait_ge(fc_top_done, 2 * at.f_full + 2)
                dve.scalar_tensor_tensor(out=neg_max_fc[:, :], in0=neg_top_fc[:, :], scalar=SLOPE,
                                         in1=neg_top_fc[:, :], op0=ALU.mult, op1=ALU.min).then_inc(full_f_done, 1)

            def evacuate(at, n, side, kind, j):
                if kind in "hi":
                    h, cols = H_OF[side], h_cols(side, kind)
                    dve.wait_ge(u_hi, at.split + at.splits(n) + 1)
                    ins = dve.tensor_tensor(h[:, 1, j, cols], proj[:, n % 2, 0:feat], h[:, 0, j, cols].bitcast(F32),
                                            ALU.subtract)
                    if kind == "h":
                        ins = dve.tensor_copy(fcol[:, F_OF[side], j, :], proj[:, n % 2, feat:feat + 3])
                    ins.then_inc(u_free[n % 2], 1)
                elif kind == "g":
                    add_r(at, n, j)
                elif by_scalar(at, n):
                    pass
                elif kind == "x":
                    unit(at, n, xT[:, j % 2, (j // 2) * HALF:(j // 2 + 1) * HALF])
                elif kind == "m":
                    dst, bias, m, half = block_place(side, j)
                    dve.wait_ge(u_done, at.unit + n + 1)
                    dve.tensor_scalar(dst[:, m, half * HALF:(half + 1) * HALF], proj[:, n % 2, :], bias[:, m:m + 1], 0.0,
                                      ALU.add, ALU.max).then_inc(u_free[n % 2], 1)
                elif kind == "r":
                    unit(at, n, f2b[:, F_OF[side], j * HALF:(j + 1) * HALF])
                elif kind == "o":
                    unit(at, n, o_nat[:, 2 * j:2 * j + 2, :].rearrange("p t f -> p (t f)"))
                if (kind, j) == ("r", 1):
                    if side == "D":
                        full_max(at, n + 1)
                    else:
                        f_whole(at, n + 1, graph_f_done if side == "F" else hand_f_done)

            def step(at, s, att, nxt):
                sc = at_distance(at, s + 3, nxt) if att else None
                first = sc if sc and nxt and s == NT - 3 else None
                if first:
                    sc = None
                summed, exped, whole = (at_distance(at, s - d) for d in (1, 2, 3))
                if sc:
                    score(*sc)
                masked = sc[1:] if sc and sc[0] != "A" else None
                if summed:
                    row_scale(*summed[1:])
                if masked:
                    dve.wait_ge(leaky_done, masked[0].masked + masked[1] + 1)
                if not summed:
                    if masked:
                        dve.tensor_copy(spare[:, 0:1], minus_one[:, :])
                elif summed[0] == "B":
                    add_x(*summed[1:])
                else:
                    elu_parts(*summed)
                if masked:
                    masked_score(*masked)
                due = None
                if summed and summed[0] == "B":
                    own, t = due = summed[1:]
                    dve.wait_ge(acc_free, own.tile + t + 1)
                    dve.bn_stats(stats[:, t, :], x1[:, t, :]).then_inc(bst_done, 1)
                if exped and exped[0] != "B":
                    elu_sum(*exped)
                if masked:
                    minus_max(*masked)
                if exped and exped[0] == "E":
                    own, t = due = exped[1:]
                    block_out(own, t)
                    dve.wait_ge(sum_done, own.resid + t + 1)
                    dve.bn_stats(stats[:, t, :], x1_res[:, t, :]).then_inc(bst_done, 1)
                if due:
                    dve.wait_ge(bst_done, due[0].masked + due[1] + 1)
                if exped and exped[0] == "B":
                    normed(*exped[1:], x1[:, exped[2], :])
                elif whole and whole[0] == "E":
                    normed(*whole[1:], x1_res[:, whole[2], :])
                elif due:
                    dve.tensor_copy(spare[:, 0:1], minus_one[:, :])
                if due:
                    dve.bn_aggr(mv[:, due[1], :], stats[:, due[1], :]).then_inc(stat_done, 1)
                if first:
                    whole_score(*first)

            def phase(at, nxt):
                for s, att, early, late in steps_of(at):
                    step(at, s, att, nxt)
                    if at.p == "D" and s == 1:
                        other_score_columns()
                    for unit_of in early:
                        evacuate(at, *unit_of)
                    lo = at_distance(at, s + 2, nxt) if att else None
                    if lo:
                        turned_lo(*lo)
                    for unit_of in late:
                        evacuate(at, *unit_of)

            def ahead(name, at):
                if name == "B":
                    make_mask()
                for t in range(3):
                    if t == 2:
                        turned_lo(name, at, 0)
                        turned_lo(name, at, 1)
                    whole_score(name, at, t)

            walk(dve, batches, phase, ahead)


def kernel(**inputs):
    import numpy as np
    import concourse.bacc as bacc
    from concourse.bass_utils import run_bass_kernel_spmd

    order = ["x", "adj", "L0_gnn_W", "L0_gnn_a", "L1_gnn_mlp1_w", "L1_gnn_mlp1_b", "L1_gnn_mlp2_w", "L1_gnn_mlp2_b",
             "L1_gnn_W_fc", "L1_gnn_a_fc", "L1_gnn_W_hand", "L1_gnn_a_hand"]
    nc = bacc.Bacc("TRN2", target_bir_lowering=False, num_devices=1)
    arrays, args = {}, []
    for name in order:
        a = np.ascontiguousarray(inputs[name])
        arrays[f"in_{name}"] = a
        args.append(nc.dram_tensor(f"in_{name}", a.shape, mybir.dt.from_np(a.dtype), kind="ExternalInput").ap())
    out = nc.dram_tensor("out_x", arrays["in_x"].shape, F32, kind="ExternalOutput").ap()
    build(nc, *args, out)
    return run_bass_kernel_spmd(nc, [arrays], core_ids=[0]).results[0]["out_x"]
```
